# Optimizing a Trainium2 kernel written in Bass

```python
import numpy as np
import jax
import jax.numpy as jnp

def _softmax(x, axis=-1):
    return jax.nn.softmax(x, axis=axis)

def _gelu(x):
    return jax.nn.gelu(x, approximate=True)

def _silu(x):
    return jax.nn.silu(x)

def _sigmoid(x):
    return jax.nn.sigmoid(x)

def _layernorm(x, axis=-1, eps=1e-05):
    m = jnp.mean(x, axis=axis, keepdims=True)
    v = jnp.var(x, axis=axis, keepdims=True)
    return (x - m) / jnp.sqrt(v + eps)

def _scatter_add(tgt, idx, src, axis=0):
    return tgt.at[idx].add(src)

def _segment_sum(src, seg, n):
    return jax.ops.segment_sum(src, seg, n)
kernel_name = 'mk_rec_standalone_d1_rec_r8_043d27'

def setup_inputs(seed: int=0):
    np.random.seed(seed)
    _w = jnp.asarray

    def _rec_inputs():
        import jax
        import jax.numpy as jnp
        _rk = jax.random.key(seed)
        r_numerical_input = -0.00299038 + 0.997414 * jax.random.normal(jax.random.fold_in(_rk, 1), (2048, 13), jnp.float32)
        r_categorical_input = jnp.stack([jax.random.randint(jax.random.fold_in(jax.random.fold_in(_rk, 2), 0), (2048,), 9, 6249, jnp.int32), jax.random.randint(jax.random.fold_in(jax.random.fold_in(_rk, 2), 1), (2048,), 2, 49994, jnp.int32), jax.random.randint(jax.random.fold_in(jax.random.fold_in(_rk, 2), 2), (2048,), 2, 49982, jnp.int32), jax.random.randint(jax.random.fold_in(jax.random.fold_in(_rk, 2), 3), (2048,), 7, 49995, jnp.int32), jax.random.randint(jax.random.fold_in(jax.random.fold_in(_rk, 2), 4), (2048,), 19, 6250, jnp.int32), jax.random.randint(jax.random.fold_in(jax.random.fold_in(_rk, 2), 5), (2048,), 6, 6250, jnp.int32), jax.random.randint(jax.random.fold_in(jax.random.fold_in(_rk, 2), 6), (2048,), 0, 6250, jnp.int32), jax.random.randint(jax.random.fold_in(jax.random.fold_in(_rk, 2), 7), (2048,), 6, 49999, jnp.int32), jax.random.randint(jax.random.fold_in(jax.random.fold_in(_rk, 2), 8), (2048,), 6, 49997, jnp.int32), jax.random.randint(jax.random.fold_in(jax.random.fold_in(_rk, 2), 9), (2048,), 6, 49967, jnp.int32), jax.random.randint(jax.random.fold_in(jax.random.fold_in(_rk, 2), 10), (2048,), 2, 6250, jnp.int32), jax.random.randint(jax.random.fold_in(jax.random.fold_in(_rk, 2), 11), (2048,), 2, 49990, jnp.int32), jax.random.randint(jax.random.fold_in(jax.random.fold_in(_rk, 2), 12), (2048,), 7, 49990, jnp.int32), jax.random.randint(jax.random.fold_in(jax.random.fold_in(_rk, 2), 13), (2048,), 3, 49993, jnp.int32), jax.random.randint(jax.random.fold_in(jax.random.fold_in(_rk, 2), 14), (2048,), 8, 49991, jnp.int32), jax.random.randint(jax.random.fold_in(jax.random.fold_in(_rk, 2), 15), (2048,), 1, 49998, jnp.int32), jax.random.randint(jax.random.fold_in(jax.random.fold_in(_rk, 2), 16), (2048,), 11, 49997, jnp.int32), jax.random.randint(jax.random.fold_in(jax.random.fold_in(_rk, 2), 17), (2048,), 5, 49995, jnp.int32), jax.random.randint(jax.random.fold_in(jax.random.fold_in(_rk, 2), 18), (2048,), 1, 6250, jnp.int32), jax.random.randint(jax.random.fold_in(jax.random.fold_in(_rk, 2), 19), (2048,), 4, 49987, jnp.int32), jax.random.randint(jax.random.fold_in(jax.random.fold_in(_rk, 2), 20), (2048,), 11, 6249, jnp.int32), jax.random.randint(jax.random.fold_in(jax.random.fold_in(_rk, 2), 21), (2048,), 2, 6250, jnp.int32), jax.random.randint(jax.random.fold_in(jax.random.fold_in(_rk, 2), 22), (2048,), 2, 49995, jnp.int32), jax.random.randint(jax.random.fold_in(jax.random.fold_in(_rk, 2), 23), (2048,), 0, 49993, jnp.int32), jax.random.randint(jax.random.fold_in(jax.random.fold_in(_rk, 2), 24), (2048,), 9, 49998, jnp.int32), jax.random.randint(jax.random.fold_in(jax.random.fold_in(_rk, 2), 25), (2048,), 0, 49982, jnp.int32)], axis=1)
        return (r_numerical_input, r_categorical_input)
    r_numerical_input, r_categorical_input = _rec_inputs()

    def _L0_rec_setup():
        import jax, jax.numpy as jnp
        import numpy as np
        B, NT, V, E = (1024, 26, 6250, 90)
        NUM_NUM = 13
        D = NT * E + NUM_NUM
        L1, L2, L3 = (1024, 512, 256)
        F = D + L3
        N_CROSS = 3
        EPS = 1e-05

        def _bn(x, g, b):
            mu = jnp.mean(x, axis=0)
            var = jnp.var(x, axis=0)
            return (x - mu) * jax.lax.rsqrt(var + EPS) * g + b
        key = jax.random.key(seed)
        ks = jax.random.split(key, 16)
        inp = {}
        inp['categorical_input'] = jax.random.randint(ks[0], (B, NT), 0, V, dtype=jnp.int64)
        inp['numerical_input'] = jax.random.normal(ks[1], (B, NUM_NUM), dtype=jnp.float32)
        inp['emb_tables'] = jax.random.normal(ks[2], (NT, V, E), dtype=jnp.float32) * 0.05
        inp['cross_alphas'] = jax.random.normal(ks[3], (N_CROSS, D), dtype=jnp.float32) * (1.0 / np.sqrt(D))
        inp['cross_bias'] = jnp.zeros((N_CROSS, D), dtype=jnp.float32)
        inp['w1'] = jax.random.normal(ks[4], (L1, D), dtype=jnp.float32) * (1.0 / np.sqrt(D))
        inp['b1'] = jnp.zeros((L1,), dtype=jnp.float32)
        inp['g1'] = jnp.ones((L1,), dtype=jnp.float32)
        inp['be1'] = jnp.zeros((L1,), dtype=jnp.float32)
        inp['w2'] = jax.random.normal(ks[5], (L2, L1), dtype=jnp.float32) * (1.0 / np.sqrt(L1))
        inp['b2'] = jnp.zeros((L2,), dtype=jnp.float32)
        inp['g2'] = jnp.ones((L2,), dtype=jnp.float32)
        inp['be2'] = jnp.zeros((L2,), dtype=jnp.float32)
        inp['w3'] = jax.random.normal(ks[6], (L3, L2), dtype=jnp.float32) * (1.0 / np.sqrt(L2))
        inp['b3'] = jnp.zeros((L3,), dtype=jnp.float32)
        inp['bn_g'] = jnp.ones((F,), dtype=jnp.float32)
        inp['bn_b'] = jnp.zeros((F,), dtype=jnp.float32)
        inp['wf'] = jax.random.normal(ks[7], (1, F), dtype=jnp.float32) * (1.0 / np.sqrt(F))
        inp['bf'] = jnp.zeros((1,), dtype=jnp.float32)
        return inp
    _L0_rec_all = _L0_rec_setup()
    _L0_rec_in = {k: v for k, v in _L0_rec_all.items() if k in ('emb_tables', 'cross_alphas', 'cross_bias', 'w1', 'b1', 'g1', 'be1', 'w2', 'b2', 'g2', 'be2', 'w3', 'b3', 'bn_g', 'bn_b', 'wf', 'bf')}
    del _L0_rec_all
    return {'r_numerical_input': r_numerical_input, 'r_categorical_input': r_categorical_input, 'L0_rec_emb_tables': _L0_rec_in['emb_tables'], 'L0_rec_cross_alphas': _L0_rec_in['cross_alphas'], 'L0_rec_cross_bias': _L0_rec_in['cross_bias'], 'L0_rec_w1': _L0_rec_in['w1'], 'L0_rec_b1': _L0_rec_in['b1'], 'L0_rec_g1': _L0_rec_in['g1'], 'L0_rec_be1': _L0_rec_in['be1'], 'L0_rec_w2': _L0_rec_in['w2'], 'L0_rec_b2': _L0_rec_in['b2'], 'L0_rec_g2': _L0_rec_in['g2'], 'L0_rec_be2': _L0_rec_in['be2'], 'L0_rec_w3': _L0_rec_in['w3'], 'L0_rec_b3': _L0_rec_in['b3'], 'L0_rec_bn_g': _L0_rec_in['bn_g'], 'L0_rec_bn_b': _L0_rec_in['bn_b'], 'L0_rec_wf': _L0_rec_in['wf'], 'L0_rec_bf': _L0_rec_in['bf']}

def reference(r_numerical_input, r_categorical_input, L0_rec_emb_tables, L0_rec_cross_alphas, L0_rec_cross_bias, L0_rec_w1, L0_rec_b1, L0_rec_g1, L0_rec_be1, L0_rec_w2, L0_rec_b2, L0_rec_g2, L0_rec_be2, L0_rec_w3, L0_rec_b3, L0_rec_bn_g, L0_rec_bn_b, L0_rec_wf, L0_rec_bf):
    import jax
    import jax.numpy as jnp

    def _L0_rec_ref(categorical_input, numerical_input, emb_tables, cross_alphas, cross_bias, w1, b1, g1, be1, w2, b2, g2, be2, w3, b3, bn_g, bn_b, wf, bf):
        import jax, jax.numpy as jnp
        import numpy as np
        B, NT, V, E = (1024, 26, 6250, 90)
        NUM_NUM = 13
        D = NT * E + NUM_NUM
        L1, L2, L3 = (1024, 512, 256)
        F = D + L3
        N_CROSS = 3
        EPS = 1e-05

        def _bn(x, g, b):
            mu = jnp.mean(x, axis=0)
            var = jnp.var(x, axis=0)
            return (x - mu) * jax.lax.rsqrt(var + EPS) * g + b
        emb = emb_tables[jnp.arange(NT)[None, :], categorical_input]
        x = jnp.concatenate([emb.reshape(emb.shape[0], -1), numerical_input], axis=1)
        h = _bn(jax.nn.relu(x @ w1.T + b1), g1, be1)
        h = _bn(jax.nn.relu(h @ w2.T + b2), g2, be2)
        h = h @ w3.T + b3
        xc = x
        for i in range(N_CROSS):
            s = xc @ cross_alphas[i]
            xc = xc * s[:, None] + cross_bias[i] + xc
        z = jnp.concatenate([xc, h], axis=1)
        z = _bn(z, bn_g, bn_b)
        return jax.nn.sigmoid(z @ wf.T + bf)
    y = _L0_rec_ref(r_categorical_input, r_numerical_input, L0_rec_emb_tables, L0_rec_cross_alphas, L0_rec_cross_bias, L0_rec_w1, L0_rec_b1, L0_rec_g1, L0_rec_be1, L0_rec_w2, L0_rec_b2, L0_rec_g2, L0_rec_be2, L0_rec_w3, L0_rec_b3, L0_rec_bn_g, L0_rec_bn_b, L0_rec_wf, L0_rec_bf)
    return y

_drawn_inputs = setup_inputs


def setup_inputs(seed=0):
    import zlib

    import numpy as np

    out = dict(_drawn_inputs(seed))
    spreads = {'L0_rec_cross_bias': (0.0, 0.1),
     'L0_rec_b1': (0.0, 0.1),
     'L0_rec_g1': (1.0, 0.539),
     'L0_rec_be1': (0.0, 0.8),
     'L0_rec_b2': (0.0, 0.8),
     'L0_rec_g2': (1.0, 0.6),
     'L0_rec_be2': (0.0, 0.8),
     'L0_rec_b3': (0.0, 0.8),
     'L0_rec_bn_g': (1.0, 0.2),
     'L0_rec_bn_b': (0.0, 0.337)}
    factors = {}
    for name, (base, spread) in spreads.items():
        noise = np.random.default_rng([zlib.crc32(name.encode()), seed]).standard_normal(out[name].shape)
        drawn = base * np.exp(spread * noise) if base else spread * noise
        out[name] = jnp.asarray(drawn.astype(out[name].dtype))
    for name, factor in factors.items():
        out[name] = (out[name] * factor).astype(out[name].dtype)
    return out
```

```python
def wide_cross_mlp(nc, cat, num, table, vec, const, w1t, w2t, w3t, out):
    from contextlib import ExitStack

    import concourse.bass as bass
    from concourse import mybir

    f32, i32 = mybir.dt.float32, mybir.dt.int32
    ALU = mybir.AluOpType
    ACT = mybir.ActivationFunctionType
    ds = bass.ds

    PT = 128
    NT, V, E = table.shape
    B, NUM = num.shape
    D = NT * E + NUM
    TILES = B // PT
    C = 2 * PT
    CHUNKS = B // C
    KT = -(-D // PT)
    DP = KT * PT
    L1, L2, L3 = w1t.shape[2], w2t.shape[2], w3t.shape[2]
    M1, M2, M3 = L1 // PT, L2 // PT, L3 // PT
    NB = 512
    N2 = B // NB
    CB = NB // C
    GROUPS = -(-KT // 2)
    HALF = -(-KT // 2)
    SLOTS = 4
    BN = 6
    EPS = 1e-05
    ACCS = 4
    table_rows = table.rearrange("a b c -> (a b) c")

    x_spill = nc.dram_tensor("x_spill", (B, NT * E), f32).ap()
    h1_spill = nc.dram_tensor("h1_spill", (CHUNKS, PT, M1 * C), f32).ap()

    ctx = ExitStack()
    with ctx:
        def sb(name, shape, dt=f32):
            return ctx.enter_context(nc.sbuf_tensor(name, shape, dt))

        def pb(name, shape):
            return ctx.enter_context(nc.psum_tensor(name, shape, f32))

        def sem(name):
            return ctx.enter_context(nc.semaphore(name))

        w1_sb = sb("w1_sb", [PT, KT * L1])
        xT_sb = sb("xT_sb", [PT, 2 * KT * C])
        nat = sb("nat", [PT, SLOTS, DP])
        h1_stage = sb("h1_stage", [PT, 2 * M1 * C])
        u_sb = sb("u_sb", [PT, HALF * C])
        w2_sb = sb("w2_sb", [PT, M1, L2])
        w1 = w1_sb[:, :].rearrange("p (k m) -> p k m", k=KT)
        xT = xT_sb[:, :].rearrange("p (b k c) -> p b k c", b=2, k=KT)
        h1s = h1_stage[:, :].rearrange("p (b m c) -> p b m c", b=2, m=M1)
        u = u_sb[:, :].rearrange("p (k c) -> p k c", k=HALF)
        h1T = w1_sb[:, 0:M1 * B].rearrange("p (n b m c) -> p n b m c", n=N2, b=CB, m=M1)
        h2T = xT_sb[:, 0:M2 * B].rearrange("p (m r) -> p m r", m=M2)
        h3T = h1_stage[:, 0:M3 * B].rearrange("p (m r) -> p m r", m=M3)
        w3_sb = w1_sb[:, M1 * B:M1 * B + M2 * L3].rearrange("p (k m) -> p k m", k=M2)
        a_row = u_sb[:, 0:DP]
        raw_f, wrap, ixf = (u_sb[:, j * TILES * NT:(j + 1) * TILES * NT].rearrange("p (t f) -> p t f", t=TILES)
                            for j in range(3))
        raw = raw_f.bitcast(i32)

        vec_sb = sb("vec_sb", [PT, vec.shape[1]])
        const_sb = sb("const_sb", [PT, const.shape[1]])
        ident = const_sb[:, 0:PT]
        table_base = const_sb[:, PT:PT + NT]
        ones = sb("ones", [PT, PT])
        index = sb("index", [PT, TILES, NT], i32)
        index_slot = sb("index_slot", [PT, SLOTS, NT], i32)
        cc_part = sb("cc_part", [PT, 3])
        cc_tmp = sb("cc_tmp", [PT, 3, KT])
        cc = sb("cc", [PT, 3])
        row = sb("row", [PT, 2, 3, 2])
        rows = sb("rows", [PT, 3, TILES])
        ra = sb("ra", [PT, 2])
        re_ = sb("re_", [PT, 2])
        rt = sb("rt", [PT, 2])
        rq = sb("rq", [PT, 2])
        r1 = sb("r1", [PT, 2])
        r2 = sb("r2", [PT, 2])
        r3 = sb("r3", [PT, 2])
        y_stats = sb("y_stats", [PT, KT, CHUNKS * BN])
        h1_stats = sb("h1_stats", [PT, M1, CHUNKS * BN])
        h2_stats = sb("h2_stats", [PT, M2, N2 * BN])
        h3_stats = sb("h3_stats", [PT, M3, N2 * BN])
        mvy = sb("mvy", [PT, KT, 2])
        mv1 = sb("mv1", [PT, M1, 2])
        mv2 = sb("mv2", [PT, M2, 2])
        mv3 = sb("mv3", [PT, M3, 2])
        bn_tmp = sb("bn_tmp", [PT, 5, KT])
        ay = sb("ay", [PT, KT])
        a1 = sb("a1", [PT, M1])
        c1 = sb("c1", [PT, M1])
        a2 = sb("a2", [PT, M2])
        c2 = sb("c2", [PT, M2])
        a3 = sb("a3", [PT, M3])
        bias2 = sb("bias2", [PT, M2])
        bias3 = sb("bias3", [PT, M3])
        fin_part = sb("fin_part", [PT, 3])
        fin_tmp = sb("fin_tmp", [PT, 4, KT])
        fin_h = sb("fin_h", [PT, 3, M3])
        fin_sum = sb("fin_sum", [PT, 4])
        fin_c = sb("fin_c", [PT, 3])
        xa = sb("xa", [PT, TILES])
        z1 = sb("z1", [PT, TILES])
        z2 = sb("z2", [PT, TILES])
        z3 = sb("z3", [PT, TILES])
        z4 = sb("z4", [PT, TILES])
        zT = sb("zT", [TILES, PT])

        at = [0]

        def take(n):
            at[0] += n
            return vec_sb[:, at[0] - n:at[0]]

        alpha = take(3 * KT).rearrange("p (k i) -> p k i", i=3)
        b0, b1x, b2x = take(KT), take(KT), take(KT)
        gy, by, wy = take(KT), take(KT), take(KT)
        b1, g1, e1 = take(M1), take(M1), take(M1)
        b2, g2, e2 = take(M2), take(M2), take(M2)
        b3, g3, e3, w_h = take(M3), take(M3), take(M3), take(M3)
        bf = take(1)

        tp = [pb(f"tp{i}", [PT, NB]) for i in range(2)]
        acc = [pb(f"acc{i}", [PT, NB]) for i in range(ACCS)]
        spread = pb("spread", [PT, 2 * NB])
        DOT0 = 3 * C

        s_vec = sem("s_vec")
        s_raw = sem("s_raw")
        s_w1 = sem("s_w1")
        s_w2 = sem("s_w2")
        s_w3 = sem("s_w3")
        s_ones = sem("s_ones")
        s_dve = sem("s_dve")
        s_row = sem("s_row")
        s_index = sem("s_index")
        s_slot = sem("s_slot")
        s_started = sem("s_started")
        s_moving = sem("s_moving")
        s_pad = sem("s_pad")
        s_gath = [sem(f"s_gath{s}") for s in range(SLOTS)]
        s_num = [sem(f"s_num{s}") for s in range(SLOTS)]
        s_spill = [sem(f"s_spill{s}") for s in range(SLOTS)]
        s_tp = sem("s_tp")
        s_xT = sem("s_xT")
        s_cc_in = sem("s_cc_in")
        s_cc_ps = sem("s_cc_ps")
        s_dots = sem("s_dots")
        s_rownum = sem("s_rownum")
        s_spread = sem("s_spread")
        s_stats = sem("s_stats")
        s_acc = sem("s_acc")
        s_h1 = sem("s_h1")
        s_bn1 = sem("s_bn1")
        s_h1out = [sem(f"s_h1out{p}") for p in range(2)]
        s_var = sem("s_var")
        s_root = sem("s_root")
        s_ay = sem("s_ay")
        s_afull = sem("s_afull")
        s_arow = sem("s_arow")
        s_h1in = [sem(f"s_h1in{n}") for n in range(N2)]
        s_c1 = sem("s_c1")
        s_shift2 = sem("s_shift2")
        s_w2f = sem("s_w2f")
        s_bias2 = sem("s_bias2")
        s_acc2 = sem("s_acc2")
        s_h2 = sem("s_h2")
        s_c2 = sem("s_c2")
        s_shift3 = sem("s_shift3")
        s_w3f = sem("s_w3f")
        s_bias3 = sem("s_bias3")
        s_acc3 = sem("s_acc3")
        s_h3 = sem("s_h3")
        s_xin = [sem(f"s_xin{s}") for s in range(SLOTS)]
        s_xa = sem("s_xa")
        s_fin_in = sem("s_fin_in")
        s_a3 = sem("s_a3")
        s_fin_ps = sem("s_fin_ps")
        s_z = sem("s_z")
        s_sig = sem("s_sig")
        s_zT = sem("s_zT")
        s_zo = sem("s_zo")
        s_out = sem("s_out")

        block = ctx.enter_context(nc.Block())

        @block.sync
        def _(sp):
            sp.dma_start(raw[:, :, :], cat).then_inc(s_raw, 16)
            sp.dma_start(vec_sb[:, :], vec).then_inc(s_vec, 16)
            sp.dma_start(const_sb[:, :], const).then_inc(s_vec, 16)
            for s in range(SLOTS):
                sp.sem_inc(s_spill[s], 16)
            for p in range(2):
                sp.sem_inc(s_h1out[p], 16)

            def numerical(i, s):
                sp.wait_ge(s_tp, GROUPS * (2 * i + s // 2 + 1))
                sp.wait_ge(s_spill[s], 16 * i + 16)
                sp.sem_inc(s_moving, 1)
                sp.dma_start(nat[:, s, NT * E:D], num[ds((i * SLOTS + s) * PT, PT), :]).then_inc(s_num[s], 16)

            def spill(i, s):
                sp.wait_ge(s_gath[s], 16 * NT * (i + 1))
                sp.sem_inc(s_moving, 1)
                sp.dma_start(x_spill[ds((i * SLOTS + s) * PT, PT), :], nat[:, s, 0:NT * E]).then_inc(s_spill[s], 16)

            def h1_out(c, p):
                sp.wait_ge(s_h1, ACCS + M1 * (c + 1))
                sp.sem_inc(s_moving, 1)
                sp.dma_start(h1_spill[ds(c, 1), :, :].rearrange("o p n -> (o p) n"),
                             h1s[:, p, :, :].rearrange("p m c -> p (m c)")).then_inc(s_h1out[p], 16)

            sp.wait_ge(s_pad, 1)
            for s in range(SLOTS):
                numerical(0, s)
            sp.dma_start(w1[:, :, :], w1t).then_inc(s_w1, 16)
            sp.dma_start(w2_sb[:, :, :], w2t).then_inc(s_w2, 16)
            PAIRS = CHUNKS // 2
            for s in range(SLOTS):
                spill(0, s)
            with sp.Fori(0, PAIRS - 1) as i:
                numerical(i + 1, 0)
                numerical(i + 1, 1)
                h1_out(2 * i, 0)
                numerical(i + 1, 2)
                numerical(i + 1, 3)
                spill(i + 1, 0)
                spill(i + 1, 1)
                h1_out(2 * i + 1, 1)
                spill(i + 1, 2)
                spill(i + 1, 3)

            def x_in(t):
                s = t % SLOTS
                if t < SLOTS:
                    sp.wait_ge(s_tp, GROUPS * (2 + CHUNKS))
                    for q in range(SLOTS):
                        sp.wait_ge(s_spill[q], 16 + 16 * TILES // SLOTS)
                else:
                    sp.wait_ge(s_xa, t - SLOTS + 1)
                rows_t = slice(t * PT, (t + 1) * PT)
                sp.dma_start(nat[:, s, 0:NT * E], x_spill[rows_t, :]).then_inc(s_xin[s], 16)
                sp.dma_start(nat[:, s, NT * E:D], num[rows_t, :]).then_inc(s_xin[s], 16)

            h1_out(CHUNKS - 2, 0)
            for t in range(SLOTS):
                x_in(t)
            h1_out(CHUNKS - 1, 1)
            sp.wait_ge(s_acc, M1 * (2 + CHUNKS))
            for p in range(2):
                sp.wait_ge(s_h1out[p], 16 + 16 * PAIRS)
            for n in range(N2):
                for b in range(CB):
                    sp.dma_start(h1T[:, n, b, :, :].rearrange("p m c -> p (m c)"),
                                 h1_spill[n * CB + b, :, :]).then_inc(s_h1in[n], 16)
            sp.dma_start(w3_sb[:, :, :], w3t).then_inc(s_w3, 16)
            for t in range(SLOTS, TILES):
                x_in(t)
            sp.wait_ge(s_zo, 1)
            sp.dma_start(out.rearrange("(t p) o -> t (p o)", p=PT), zT[:, :]).then_inc(s_out, 16)
            sp.wait_ge(s_out, 16)

        @block.gpsimd
        def _(pool):
            nc.gpsimd.memset(nat[:, :, NT * E:DP], 0.0).then_inc(s_pad, 1)
            pool.wait_ge(s_index, 1)
            with pool.Fori(0, TILES // SLOTS) as i:
                for s in range(SLOTS):
                    pool.wait_ge(s_tp, GROUPS * (2 * i + s // 2 + 1))
                    pool.wait_ge(s_spill[s], 16 * i + 16)
                    nc.gpsimd.tensor_copy(index_slot[:, s, :],
                                          index[:, ds(i * SLOTS + s, 1), :].rearrange("p a f -> p (a f)")
                                          ).then_inc(s_slot, 1)
                    pool.wait_ge(s_slot, SLOTS * i + s + 1)
                    pool.sem_inc(s_started, 1)
                    for f in range(NT):
                        nc.gpsimd.indirect_dma_start(
                            nat[:, s, f * E:(f + 1) * E], None, table_rows,
                            bass.IndirectOffsetOnAxis(ap=index_slot[:, s, f:f + 1], axis=0),
                        ).then_inc(s_gath[s], 16)

        PLAN = {3: 2, 4: 2, 5: 3, 6: 3}

        def width(g):
            return min(2, KT - 2 * g)

        @block.scalar
        def _(act):
            act.sem_inc(s_xT, 2)
            act.sem_inc(s_h1, ACCS)

            def copy_xT(c, p, g):
                act.wait_ge(s_tp, GROUPS * (c + 2) + g + 1)
                if g == 0:
                    act.wait_ge(s_acc, M1 * (c + 1))
                    act.wait_ge(s_stats, c + 1)
                n = width(g)
                nc.scalar.copy(xT[:, p, 2 * g:2 * g + n, :].rearrange("p k c -> p (k c)"),
                               tp[g % 2][:, 0:n * C]).then_inc(s_xT, 1)

            def relu_h1(c, p, m):
                act.wait_ge(s_acc, M1 * (c + 2) + m + 1)
                if m == 0:
                    act.wait_ge(s_h1out[p], 16 * ((c - p) // 2) + 16 if isinstance(c, int) else (c - p) * 8 + 16)
                    act.wait_ge(s_bn1, c + 1)
                nc.scalar.activation(h1s[:, p, m, :], acc[m % ACCS][:, 0:C],
                                     ACT.Relu, bias=b1[:, m:m + 1]).then_inc(s_h1, 1)

            def chunk(c, p, ahead):
                g = 0
                for m in range(M1):
                    relu_h1(c, p, m)
                    if ahead:
                        for _ in range(PLAN.get(m, 0)):
                            copy_xT(c + 1, 1 - p, g)
                            g += 1

            def root(n, k):
                act.wait_ge(s_var, n)
                nc.scalar.activation(bn_tmp[:, 1, 0:k], bn_tmp[:, 0, 0:k], ACT.Sqrt).then_inc(s_root, 1)

            act.wait_ge(s_vec, 32)
            for g in range(GROUPS):
                copy_xT(0, 0, g)
            with act.Fori(0, CHUNKS // 2 - 1) as i:
                chunk(2 * i, 0, True)
                chunk(2 * i + 1, 1, True)
            chunk(CHUNKS - 2, 0, True)
            for m in range(M1):
                relu_h1(CHUNKS - 1, 1, m)
                if m == 5:
                    root(1, KT)
            for g in range(-(-KT // 8)):
                n = min(8, KT - 8 * g)
                for h in range(-(-n // 4)):
                    w = min(4, n - 4 * h)
                    act.wait_ge(s_afull, 2 * g + h + 1)
                    nc.scalar.copy(a_row[:, (8 * g + 4 * h) * PT:(8 * g + 4 * h + w) * PT],
                                   tp[h][:, 0:w * PT]).then_inc(s_arow, 1)
            root(2, M1)
            act.wait_ge(s_c1, 1)
            act.wait_ge(s_shift2, 1)
            for k in range(1, M1, 2):
                nc.scalar.activation(w2_sb[:, k, :], w2_sb[:, k, :], ACT.Copy,
                                     scale=a1[:, k:k + 1]).then_inc(s_w2f, 1)
            act.sem_inc(s_h2, ACCS)
            act.wait_ge(s_bias2, 1)
            with act.Fori(0, N2) as n:
                for m in range(M2):
                    act.wait_ge(s_acc2, M2 * n + m + 1)
                    nc.scalar.activation(h2T[:, m, ds(n * NB, NB)], acc[m][:, :], ACT.Relu,
                                         bias=bias2[:, m:m + 1]).then_inc(s_h2, 1)
            root(3, M2)
            act.wait_ge(s_c2, 1)
            act.wait_ge(s_shift3, 1)
            for k in range(1, M2, 2):
                nc.scalar.activation(w3_sb[:, k, :], w3_sb[:, k, :], ACT.Copy,
                                     scale=a2[:, k:k + 1]).then_inc(s_w3f, 1)
            act.sem_inc(s_h3, ACCS)
            act.wait_ge(s_bias3, 1)
            with act.Fori(0, N2 // 2) as n:
                for q in range(2 * M3):
                    act.wait_ge(s_acc3, 2 * M3 * n + q + 1)
                    nc.scalar.activation(h3T[:, q % M3, ds(n * (2 * NB) + (q // M3) * NB, NB)], acc[q][:, :],
                                         ACT.Identity, bias=bias3[:, q % M3:q % M3 + 1]).then_inc(s_h3, 1)
            root(4, M3)
            act.wait_ge(s_z, 1)
            nc.scalar.activation(z1[:, :], z4[:, :], ACT.Sigmoid).then_inc(s_sig, 1)
            act.wait_ge(s_zT, 1)
            nc.scalar.copy(zT[:, :], spread[0:TILES, NB:NB + PT]).then_inc(s_zo, 1)

        @block.vector
        def _(dve):
            done = [0]

            def link(ins):
                done[0] += 1
                ins.then_inc(s_dve, 1)
                dve.wait_ge(s_dve, done[0])

            v = nc.vector
            dve.sem_inc(s_bn1, 2)
            dve.wait_ge(s_raw, 16)
            dve.wait_ge(s_vec, 32)
            link(v.tensor_copy(ixf[:, :, :], raw[:, :, :]))
            link(v.tensor_scalar(wrap[:, :, :], ixf[:, :, :], 0.0, float(V), ALU.is_lt, ALU.mult))
            link(v.tensor_tensor(ixf[:, :, :], ixf[:, :, :], wrap[:, :, :], ALU.add))
            link(v.tensor_scalar(ixf[:, :, :], ixf[:, :, :], 0.0, float(V - 1), ALU.max, ALU.min))
            v.tensor_tensor(index[:, :, :], ixf[:, :, :],
                            table_base.unsqueeze(1).broadcast_to([PT, TILES, NT]), ALU.add).then_inc(s_index, 1)
            v.memset(ones[:, :], 1.0).then_inc(s_ones, 1)
            link(v.tensor_tensor(cc_tmp[:, 0, :], b0, alpha[:, :, 1], ALU.mult))
            link(v.tensor_tensor(cc_tmp[:, 1, :], b0, alpha[:, :, 2], ALU.mult))
            link(v.tensor_tensor(cc_tmp[:, 2, :], b1x, alpha[:, :, 2], ALU.mult))
            v.reduce_sum(cc_part[:, :], cc_tmp[:, :, :], axis=mybir.AxisListType.X).then_inc(s_cc_in, 1)
            dve.wait_ge(s_cc_ps, 1)
            link(v.tensor_copy(cc[:, :], spread[:, DOT0:DOT0 + 3]))
            dve.sem_inc(s_stats, 2)

            LINKS = 17

            def chunk(c, p, steps):
                local = [0]

                def row_link(ins):
                    local[0] += 1
                    ins.then_inc(s_row, 1)
                    dve.wait_ge(s_row, LINKS * c + local[0])

                dve.wait_ge(s_dots, c + 1)
                dot = spread[:, DOT0 + 8 * p:DOT0 + 8 * p + 8].rearrange("p (j i) -> p j i", i=4)
                row_link(v.tensor_scalar(ra[:, :], dot[:, :, 0], 1.0, None, ALU.add))
                v.tensor_tensor(r2[:, :], ra[:, :], dot[:, :, 2], ALU.mult)
                row_link(v.tensor_tensor(r1[:, :], ra[:, :], dot[:, :, 1], ALU.mult))
                row_link(v.tensor_scalar(re_[:, :], r1[:, :], cc[:, 0:1], 1.0, ALU.add, ALU.add))
                row_link(v.scalar_tensor_tensor(out=r3[:, :], in0=r2[:, :], scalar=cc[:, 1:2], in1=re_[:, :],
                                                op0=ALU.add, op1=ALU.mult))
                row_link(v.tensor_scalar(rt[:, :], r3[:, :], cc[:, 2:3], 1.0, ALU.add, ALU.add))
                v.tensor_scalar(row[:, p, 2, :], rt[:, :], -1.0, None, ALU.add)
                row_link(v.tensor_tensor(rq[:, :], re_[:, :], rt[:, :], ALU.mult))
                v.tensor_scalar(row[:, p, 1, :], rq[:, :], -1.0, None, ALU.add)
                row_link(v.tensor_tensor(row[:, p, 0, :], ra[:, :], rq[:, :], ALU.mult))
                row_link(v.tensor_copy(rows[:, :, ds(2 * c, 2)], row[:, p, :, :]))
                dve.sem_inc(s_rownum, 1)
                dve.wait_ge(s_spread, c + 1)
                for lot in range(2):
                    k0 = lot * HALF
                    n = min(HALF, KT - k0)
                    row_link(v.tensor_tensor(u[:, 0:n, :], xT[:, p, k0:k0 + n, :],
                                             spread[:, 0:C].unsqueeze(1).broadcast_to([PT, n, C]), ALU.mult))
                    for q, b in ((1, b0), (2, b1x)):
                        for k in range(n):
                            last = v.scalar_tensor_tensor(
                                out=u[:, k, :], in0=spread[:, q * C:(q + 1) * C], scalar=b[:, k0 + k:k0 + k + 1],
                                in1=u[:, k, :], op0=ALU.mult, op1=ALU.add)
                        row_link(last)
                    for k in range(n):
                        last = v.bn_stats(y_stats[:, k0 + k, ds(c * BN, BN)], u[:, k, :])
                    row_link(last)
                dve.sem_inc(s_stats, 1)
                steps()
                dve.wait_ge(s_h1, ACCS + M1 * (c + 1))
                for m in range(M1):
                    last = v.bn_stats(h1_stats[:, m, ds(c * BN, BN)], h1s[:, p, m, :])
                row_link(last)
                dve.sem_inc(s_bn1, 1)
                assert local[0] == LINKS, local[0]

            def inverse_root(n, var, k):
                t = [bn_tmp[:, j, 0:k] for j in range(5)]
                link(v.tensor_scalar(t[0], var, EPS, None, ALU.add))
                dve.sem_inc(s_var, 1)
                dve.wait_ge(s_root, n)
                link(v.reciprocal(t[2], t[1]))
                link(v.tensor_tensor(t[3], t[2], t[2], ALU.mult))
                link(v.tensor_tensor(t[3], t[3], t[0], ALU.mult))
                link(v.tensor_scalar(t[3], t[3], -0.5, 1.5, ALU.mult, ALU.add))
                link(v.tensor_tensor(t[4], t[2], t[3], ALU.mult))
                return t[4]

            def aggregate(mv, stats, k):
                for j in range(k):
                    last = v.bn_aggr(mv[:, j, :], stats[:, j, :])
                link(last)

            def fold_y():
                aggregate(mvy, y_stats, KT)
                r = inverse_root(1, mvy[:, :, 1], KT)
                link(v.tensor_tensor(ay[:, :], r, gy, ALU.mult))
                link(v.tensor_tensor(ay[:, :], ay[:, :], wy, ALU.mult))
                dve.sem_inc(s_ay, 1)
                link(v.tensor_tensor(fin_tmp[:, 0, :], b0, ay[:, :], ALU.mult))
                link(v.tensor_tensor(fin_tmp[:, 1, :], b1x, ay[:, :], ALU.mult))
                link(v.tensor_tensor(fin_tmp[:, 3, :], mvy[:, :, 0], b2x, ALU.add))
                link(v.tensor_tensor(fin_tmp[:, 3, :], b2x, fin_tmp[:, 3, :], ALU.subtract))
                link(v.tensor_tensor(fin_tmp[:, 3, :], fin_tmp[:, 3, :], ay[:, :], ALU.mult))
                link(v.tensor_tensor(fin_tmp[:, 2, :], by, wy, ALU.mult))
                link(v.tensor_tensor(fin_tmp[:, 2, :], fin_tmp[:, 2, :], fin_tmp[:, 3, :], ALU.add))
                link(v.reduce_sum(fin_sum[:, 0:3], fin_tmp[:, 0:3, :], axis=mybir.AxisListType.X))

            def none():
                pass

            with dve.Fori(0, CHUNKS // 2 - 1) as i:
                chunk(2 * i, 0, none)
                chunk(2 * i + 1, 1, none)
            chunk(CHUNKS - 2, 0, none)
            chunk(CHUNKS - 1, 1, fold_y)

            def fold(n, mv, stats, k, a, c, g, e):
                aggregate(mv, stats, k)
                r = inverse_root(n, mv[:, :, 1], k)
                link(v.tensor_tensor(a[:, :], r, g, ALU.mult))
                link(v.tensor_tensor(c[:, :], mv[:, :, 0], a[:, :], ALU.mult))
                link(v.tensor_tensor(c[:, :], e, c[:, :], ALU.subtract))

            fold(2, mv1, h1_stats, M1, a1, c1, g1, e1)
            dve.sem_inc(s_c1, 1)
            dve.wait_ge(s_shift2, 1)
            link(v.tensor_tensor(bias2[:, :], spread[:, 0:M2], b2, ALU.add))
            dve.sem_inc(s_bias2, 1)
            for k in range(0, M1, 2):
                v.tensor_scalar(w2_sb[:, k, :], w2_sb[:, k, :], a1[:, k:k + 1], None, ALU.mult).then_inc(s_w2f, 1)
            dve.wait_ge(s_arow, -(-KT // 4))

            def read_out(t):
                dve.wait_ge(s_xin[t % SLOTS], 32 * (t // SLOTS + 1))
                v.tensor_tensor_reduce(out=nat[:, t % SLOTS, 0:D], in0=nat[:, t % SLOTS, 0:D], in1=a_row[:, 0:D],
                                       scale=1.0, scalar=0.0, op0=ALU.mult, op1=ALU.add,
                                       accum_out=xa[:, t:t + 1]).then_inc(s_xa, 1)

            per = TILES // N2
            for n in range(N2):
                for t in range(n * per, (n + 1) * per):
                    read_out(t)
                for m in range(M2):
                    dve.wait_ge(s_h2, ACCS + M2 * n + m + 1)
                    last = v.bn_stats(h2_stats[:, m, n * BN:(n + 1) * BN], h2T[:, m, n * NB:(n + 1) * NB])
            link(last)
            fold(3, mv2, h2_stats, M2, a2, c2, g2, e2)
            dve.sem_inc(s_c2, 1)
            dve.wait_ge(s_shift3, 1)
            link(v.tensor_tensor(bias3[:, :], spread[:, 8:8 + M3], b3, ALU.add))
            dve.sem_inc(s_bias3, 1)
            for k in range(0, M2, 2):
                v.tensor_scalar(w3_sb[:, k, :], w3_sb[:, k, :], a2[:, k:k + 1], None, ALU.mult).then_inc(s_w3f, 1)
            for n in range(N2):
                for m in range(M3):
                    dve.wait_ge(s_h3, ACCS + M3 * n + m + 1)
                    last = v.bn_stats(h3_stats[:, m, n * BN:(n + 1) * BN], h3T[:, m, n * NB:(n + 1) * NB])
            link(last)
            aggregate(mv3, h3_stats, M3)
            r = inverse_root(4, mv3[:, :, 1], M3)
            link(v.tensor_tensor(a3[:, :], r, g3, ALU.mult))
            link(v.tensor_tensor(a3[:, :], a3[:, :], w_h, ALU.mult))
            dve.sem_inc(s_a3, 1)
            link(v.tensor_tensor(fin_h[:, 0, :], mv3[:, :, 0], a3[:, :], ALU.mult))
            link(v.tensor_tensor(fin_h[:, 1, :], e3, w_h, ALU.mult))
            link(v.tensor_tensor(fin_h[:, 2, :], fin_h[:, 1, :], fin_h[:, 0, :], ALU.subtract))
            link(v.reduce_sum(fin_sum[:, 3:4], fin_h[:, 2, :], axis=mybir.AxisListType.X))
            link(v.tensor_copy(fin_part[:, 0:2], fin_sum[:, 0:2]))
            link(v.tensor_tensor(fin_part[:, 2:3], fin_sum[:, 2:3], fin_sum[:, 3:4], ALU.add))
            link(v.tensor_tensor(fin_part[:, 2:3], fin_part[:, 2:3], bf, ALU.add))
            dve.sem_inc(s_fin_in, 1)
            dve.wait_ge(s_fin_ps, 1)
            link(v.tensor_copy(fin_c[:, :], spread[:, 16:19]))
            link(v.tensor_tensor(z1[:, :], rows[:, 0, :], xa[:, :], ALU.mult))
            link(v.scalar_tensor_tensor(out=z2[:, :], in0=rows[:, 1, :], scalar=fin_c[:, 0:1], in1=z1[:, :],
                                        op0=ALU.mult, op1=ALU.add))
            link(v.scalar_tensor_tensor(out=z3[:, :], in0=rows[:, 2, :], scalar=fin_c[:, 1:2], in1=z2[:, :],
                                        op0=ALU.mult, op1=ALU.add))
            v.scalar_tensor_tensor(out=z4[:, :], in0=spread[:, 32:32 + TILES], scalar=fin_c[:, 2:3], in1=z3[:, :],
                                   op0=ALU.add, op1=ALU.add).then_inc(s_z, 1)

        @block.tensor
        def _(pe):
            mm = nc.tensor.matmul
            pe.sem_inc(s_tp, 2 * GROUPS)
            pe.sem_inc(s_acc, 2 * M1)

            def turn(c, p, i, g):
                if g == 0:
                    for j in range(2):
                        pe.wait_ge(s_gath[2 * p + j], 16 * NT * (i + 1))
                        pe.wait_ge(s_num[2 * p + j], 16 * (i + 1))
                pe.wait_ge(s_xT, GROUPS * c + g + 1)
                for k in range(width(g)):
                    for j in range(2):
                        last = nc.tensor.transpose(tp[g % 2][:, k * C + j * PT:k * C + (j + 1) * PT],
                                                   nat[:, 2 * p + j, (2 * g + k) * PT:(2 * g + k + 1) * PT], ident)
                last.then_inc(s_tp, 1)

            def dots(c, p):
                pe.wait_ge(s_xT, 2 + GROUPS * (c + 1))
                pe.wait_ge(s_stats, c + 2)
                for j in range(2):
                    o = DOT0 + 8 * p + 4 * j
                    for k in range(KT):
                        last = mm(spread[:, o:o + 3], xT[:, p, k, j * PT:(j + 1) * PT], alpha[:, k, :],
                                  start=(k == 0), stop=(k == KT - 1))
                last.then_inc(s_dots, 1)

            def spread_rows(c, p):
                pe.wait_ge(s_rownum, c + 1)
                for q in range(3):
                    for j in range(2):
                        last = mm(spread[:, q * C + j * PT:q * C + (j + 1) * PT],
                                  row[:, p, q, j:j + 1].broadcast_to([PT, PT]), ident, start=True, stop=True)
                last.then_inc(s_spread, 1)

            def chunk(c, p, ahead, nxt):
                dots(c, p)
                g = 0
                for m in range(M1):
                    pe.wait_ge(s_h1, M1 * c + m + 1)
                    for k in range(KT):
                        last = mm(acc[m % ACCS][:, 0:C], w1[:, k, m * PT:(m + 1) * PT],
                                  xT[:, p, k, :], start=(k == 0), stop=(k == KT - 1))
                    last.then_inc(s_acc, 1)
                    if m == 1:
                        spread_rows(c, p)
                    if ahead:
                        for _ in range(PLAN.get(m, 0)):
                            turn(c + 1, 1 - p, nxt, g)
                            g += 1

            pe.wait_ge(s_ones, 1)
            pe.wait_ge(s_cc_in, 1)
            mm(spread[:, DOT0:DOT0 + 3], ones[:, :], cc_part[:, :], start=True, stop=True).then_inc(s_cc_ps, 1)
            pe.wait_ge(s_vec, 32)
            pe.wait_ge(s_pad, 1)
            for g in range(GROUPS):
                turn(0, 0, 0, g)
            pe.wait_ge(s_w1, 16)
            with pe.Fori(0, CHUNKS // 2 - 1) as i:
                chunk(2 * i, 0, True, i)
                chunk(2 * i + 1, 1, True, i + 1)
            chunk(CHUNKS - 2, 0, True, CHUNKS // 2 - 1)
            chunk(CHUNKS - 1, 1, False, None)

            pe.wait_ge(s_ay, 1)
            for g in range(-(-KT // 4)):
                if g >= 2:
                    pe.wait_ge(s_arow, g - 1)
                for k in range(4 * g, min(KT, 4 * g + 4)):
                    last = mm(tp[g % 2][:, (k % 4) * PT:(k % 4 + 1) * PT],
                              ay[:, k:k + 1].broadcast_to([PT, PT]), ident, start=True, stop=True)
                last.then_inc(s_afull, 1)

            def shift(c, w, kt, mt, at_col, s_in, s_done):
                pe.wait_ge(s_in, 1)
                for m in range(mt):
                    for k in range(kt):
                        last = mm(spread[:, at_col + m:at_col + m + 1], w[:, k, m * PT:(m + 1) * PT], c[:, k:k + 1],
                                  start=(k == 0), stop=(k == kt - 1))
                last.then_inc(s_done, 1)

            pe.wait_ge(s_w2, 16)
            shift(c1, w2_sb, M1, M2, 0, s_c1, s_shift2)
            pe.wait_ge(s_w2f, M1)
            for n in range(N2):
                pe.wait_ge(s_h1in[n], 16 * CB)
                for m in range(M2):
                    pe.wait_ge(s_h2, M2 * n + m + 1)
                    for k in range(M1):
                        last = mm(acc[m][:, :], w2_sb[:, k, m * PT:(m + 1) * PT], h1T[:, n, :, k, :],
                                  start=(k == 0), stop=(k == M1 - 1))
                    last.then_inc(s_acc2, 1)
            pe.wait_ge(s_w3, 16)
            shift(c2, w3_sb, M2, M3, 8, s_c2, s_shift3)
            pe.wait_ge(s_w3f, M2)
            with pe.Fori(0, N2 // 2) as n:
                for q in range(2 * M3):
                    pe.wait_ge(s_h3, 2 * M3 * n + q + 1)
                    for k in range(M2):
                        last = mm(acc[q][:, :], w3_sb[:, k, (q % M3) * PT:(q % M3 + 1) * PT],
                                  h2T[:, k, ds(n * (2 * NB) + (q // M3) * NB, NB)],
                                  start=(k == 0), stop=(k == M2 - 1))
                    last.then_inc(s_acc3, 1)
            pe.wait_ge(s_a3, 1)
            for t in range(TILES):
                for m in range(M3):
                    mm(spread[:, 32 + t:33 + t], h3T[:, m, t * PT:(t + 1) * PT], a3[:, m:m + 1],
                       start=(m == 0), stop=(m == M3 - 1))
            pe.wait_ge(s_fin_in, 1)
            mm(spread[:, 16:19], ones[:, :], fin_part[:, :], start=True, stop=True).then_inc(s_fin_ps, 1)
            pe.wait_ge(s_sig, 1)
            nc.tensor.transpose(spread[0:TILES, NB:NB + PT], z1[:, :], ident).then_inc(s_zT, 1)


def kernel(r_numerical_input, r_categorical_input, L0_rec_emb_tables, L0_rec_cross_alphas, L0_rec_cross_bias,
           L0_rec_w1, L0_rec_b1, L0_rec_g1, L0_rec_be1, L0_rec_w2, L0_rec_b2, L0_rec_g2, L0_rec_be2,
           L0_rec_w3, L0_rec_b3, L0_rec_bn_g, L0_rec_bn_b, L0_rec_wf, L0_rec_bf):
    import numpy as np
    import concourse.bacc as bacc
    from concourse import mybir
    from concourse.bass_utils import run_bass_kernel_spmd

    P = 128

    def columns(v):
        v = np.asarray(v).reshape(-1)
        n = -(-v.shape[0] // P)
        full = np.zeros((n * P,), v.dtype)
        full[:v.shape[0]] = v
        return full.reshape(n, P).T

    def weights(w):
        w = np.asarray(w)
        kt = -(-w.shape[1] // P)
        full = np.zeros((kt * P, w.shape[0]), w.dtype)
        full[:w.shape[1]] = w.T
        return np.ascontiguousarray(full.reshape(kt, P, w.shape[0]).transpose(1, 0, 2))

    cat = np.asarray(r_categorical_input)
    tables = np.ascontiguousarray(L0_rec_emb_tables)
    nt, v_rows, e = tables.shape
    d = L0_rec_w1.shape[1]
    alphas = np.stack([columns(a) for a in np.asarray(L0_rec_cross_alphas)], axis=2).reshape(P, -1)
    bias = [columns(b) for b in np.asarray(L0_rec_cross_bias)]
    bn_g, bn_b, wf = (np.asarray(a).reshape(-1) for a in (L0_rec_bn_g, L0_rec_bn_b, L0_rec_wf))
    vec = [alphas, *bias, columns(bn_g[:d]), columns(bn_b[:d]), columns(wf[:d]),
           columns(L0_rec_b1), columns(L0_rec_g1), columns(L0_rec_be1),
           columns(L0_rec_b2), columns(L0_rec_g2), columns(L0_rec_be2),
           columns(L0_rec_b3), columns(bn_g[d:]), columns(bn_b[d:]), columns(wf[d:]), columns(L0_rec_bf)]
    base = np.broadcast_to(np.arange(nt, dtype=np.float32) * v_rows, (P, nt))
    arrays = {
        "cat": np.ascontiguousarray(cat.reshape(-1, P, nt).transpose(1, 0, 2)),
        "num": np.ascontiguousarray(r_numerical_input),
        "table": tables,
        "vec": np.ascontiguousarray(np.concatenate(vec, axis=1)),
        "const": np.ascontiguousarray(np.concatenate([np.eye(P, dtype=np.float32), base], axis=1)),
        "w1t": weights(L0_rec_w1), "w2t": weights(L0_rec_w2), "w3t": weights(L0_rec_w3),
    }
    nc = bacc.Bacc("TRN2", target_bir_lowering=False, num_devices=1)
    args = [nc.dram_tensor(name, a.shape, mybir.dt.from_np(a.dtype), kind="ExternalInput").ap()
            for name, a in arrays.items()]
    out = nc.dram_tensor("out", (cat.shape[0], 1), mybir.dt.float32, kind="ExternalOutput").ap()
    wide_cross_mlp(nc, *args, out)
    return run_bass_kernel_spmd(nc, [arrays], core_ids=[0]).results[0]["out"]
```

```python
def wide_cross_mlp(nc, cat, num, table, vec, const, w1t, w2t, w3t, out):
    from contextlib import ExitStack

    import concourse.bass as bass
    from concourse import mybir

    f32, f16, bf16, i32 = mybir.dt.float32, mybir.dt.float16, mybir.dt.bfloat16, mybir.dt.int32
    ALU = mybir.AluOpType
    ACT = mybir.ActivationFunctionType
    AX = mybir.AxisListType
    ds = bass.ds

    PT = 128
    NT, V, E = table.shape
    B, NUM = num.shape
    D = NT * E + NUM
    TILES = B // PT
    C = 2 * PT
    CHUNKS = B // C
    PAIRS = CHUNKS // 2
    KT = -(-D // PT)
    DP = KT * PT
    L1, L2, L3 = w1t.shape[2], w2t.shape[2], w3t.shape[2]
    M1, M2, M3 = L1 // PT, L2 // PT, L3 // PT
    NB = 512
    N2 = B // NB
    CB = NB // C
    GK = NB // PT
    GROUPS = -(-KT // GK)
    YK = NB // C
    YBANKS = -(-KT // YK)
    TERMS = 6
    SLOTS = 4
    XSLOTS = 3
    SHIFT = 4
    BN = 6
    EPS = 1e-05
    ROOM = 14
    NSCALE = 512.0
    TINY = 2.0 ** -100
    BIAS = 127 << 22
    EXPONENT = 0x7F800000
    ORDER = [N2 - 1] + list(range(N2 - 1))
    assert CB == 2 and NSCALE * B ** 0.5 < 2.0 ** 15
    table_rows = table.rearrange("a b c -> (a b) c")

    x_spill = nc.dram_tensor("x_spill", (B, NT * E), f32).ap()
    h1_spill = nc.dram_tensor("h1_spill", (CHUNKS - CB, PT, M1 * C), f32).ap()

    ctx = ExitStack()
    with ctx:
        def sb(name, shape, dt=f32):
            return ctx.enter_context(nc.sbuf_tensor(name, shape, dt))

        def pb(name, shape):
            return ctx.enter_context(nc.psum_tensor(name, shape, f32))

        def sem(name):
            return ctx.enter_context(nc.semaphore(name))

        W1_WORDS = KT * L1
        STAGE = 2 * M1 * C
        arena = sb("arena", [PT, W1_WORDS + STAGE])
        w1 = arena[:, 0:W1_WORDS].bitcast(f16).rearrange("p (k s m) -> p k s m", k=KT, s=2)
        w1_raw = arena[:, SHIFT * L1:(SHIFT + KT) * L1].rearrange("p (k m) -> p k m", k=KT)
        h1s = arena[:, W1_WORDS:W1_WORDS + STAGE].rearrange("p (b m c) -> p b m c", b=2, m=M1)
        assert SHIFT * L1 <= STAGE
        xT_sb = sb("xT_sb", [PT, 2 * KT * C])
        xT = xT_sb[:, :].bitcast(f16).rearrange("p (b s k c) -> p b s k c", b=2, s=2, k=KT)
        nat = sb("nat", [PT, SLOTS, DP])
        squares_sb = sb("squares_sb", [PT, (D + 1) // 2])
        squares = squares_sb[:, :].bitcast(bf16)[:, 0:D]
        b_part = sb("b_part", [PT, DP], bf16)
        r_part = sb("r_part", [PT, 2, C], bf16)
        w2 = sb("w2", [PT, 2, M1, L2], f16)
        raw_f, wrap_f = (nat[:, SLOTS - 1, j * TILES * NT:(j + 1) * TILES * NT].rearrange(
            "p (t f) -> p t f", t=TILES) for j in range(2))
        raw = raw_f.bitcast(i32)
        ixf = nat[:, SLOTS - 1, 2 * TILES * NT:3 * TILES * NT].rearrange("p (t f) -> p t f", t=TILES)
        w2_raw = xT_sb[:, 0:M1 * L2].rearrange("p (k m) -> p k m", k=M1)
        BLOCK = M1 * NB
        h1r = [arena[:, j * BLOCK:(j + 1) * BLOCK].rearrange("p (b m c) -> p b m c", b=CB, m=M1)
               for j in range(2)]
        n1 = [arena[:, (2 + j) * BLOCK:(3 + j) * BLOCK].bitcast(f16).rearrange(
            "p (s k r) -> p s k r", s=2, k=M1) for j in range(2)]
        AT3 = 4 * BLOCK
        w3_raw, w3_g = (arena[:, AT3 + j * M2 * L3:AT3 + (j + 1) * M2 * L3].rearrange(
            "p (k m) -> p k m", k=M2) for j in range(2))
        w3 = arena[:, AT3 + 2 * M2 * L3:AT3 + 3 * M2 * L3].bitcast(f16).rearrange(
            "p (s k m) -> p s k m", s=2, k=M2)
        assert AT3 + 3 * M2 * L3 <= W1_WORDS
        h2T = xT_sb[:, 0:M2 * B].rearrange("p (m r) -> p m r", m=M2)
        n2 = arena[:, 0:M2 * B].bitcast(f16).rearrange("p (s k r) -> p s k r", s=2, k=M2)
        assert M2 * B <= 2 * BLOCK
        h3T = arena[:, W1_WORDS:W1_WORDS + M3 * B].rearrange("p (m r) -> p m r", m=M3)
        a_row = nat[:, SLOTS - 1, :]

        vec_sb = sb("vec_sb", [PT, vec.shape[1]])
        const_sb = sb("const_sb", [PT, const.shape[1]])
        ident = const_sb[:, 0:PT]
        table_base = const_sb[:, PT:PT + NT]
        ones = sb("ones", [PT, PT])
        index = sb("index", [PT, TILES, NT], i32)
        index_slot = sb("index_slot", [PT, SLOTS, NT], i32)
        part1 = sb("part1", [PT, 4])
        cc = sb("cc", [PT, 3])
        al = sb("al", [PT, KT, 2, 3], f16)
        mx_w1 = sb("mx_w1", [PT, 8])
        mx = sb("mx", [PT, 4])
        bound = sb("bound", [PT, 1])
        power = sb("power", [PT, 1], i32)
        rpower = sb("rpower", [PT, 1])
        sc_al, iv_al = sb("sc_al", [PT, 1]), sb("iv_al", [PT, 1])
        sc_w1, iv_w1 = sb("sc_w1", [PT, 1]), sb("iv_w1", [PT, 1])
        sc_w2, iv_w2 = sb("sc_w2", [PT, 1]), sb("iv_w2", [PT, 1])
        sc_w3, iv_w3 = sb("sc_w3", [PT, 1]), sb("iv_w3", [PT, 1])
        sc_x = sb("sc_x", [PT, 2, 2])
        iv_h = sb("iv_h", [PT, 2, 2])
        iv_d = sb("iv_d", [PT, 2, 2])
        dot6 = sb("dot6", [PT, 2, 6])
        dot3 = sb("dot3", [PT, 2, 3])
        p_row = sb("p_row", [PT, 2, 2])
        qt_row = sb("qt_row", [PT, 2, 2])
        qt_rest = sb("qt_rest", [PT, 2, 2])
        qt_part = sb("qt_part", [PT, 2, 2 * TERMS], bf16)
        bb, bb_rest = (squares_sb[:, j * 2 * KT:(j + 1) * 2 * KT].rearrange("p (k b) -> p k b", k=KT)
                       for j in range(2))
        bb_part = squares_sb[:, 4 * KT:(4 + TERMS) * KT].bitcast(bf16).rearrange("p (k i) -> p k i", k=KT)
        cc_tmp = squares_sb[:, (4 + TERMS) * KT:(7 + TERMS) * KT].rearrange("p (i k) -> p i k", i=3)
        ident16 = sb("ident16", [PT, PT], bf16)
        rows = sb("rows", [PT, 3, TILES])
        ra, rf, rt, rq, r1, r2, r3 = (sb(f"r_{n}", [PT, 2]) for n in "aftq123")
        y_stats = sb("y_stats", [PT, KT, CHUNKS * BN])
        h1_stats = sb("h1_stats", [PT, M1, CHUNKS * BN])
        h2_stats = sb("h2_stats", [PT, M2, N2 * BN])
        h3_stats = sb("h3_stats", [PT, M3, N2 * BN])
        mvy = sb("mvy", [PT, KT, 2])
        mv1 = sb("mv1", [PT, M1, 2])
        mv2 = sb("mv2", [PT, M2, 2])
        mv3 = sb("mv3", [PT, M3, 2])
        bn_tmp = sb("bn_tmp", [PT, 5, KT])
        ay = sb("ay", [PT, KT])
        rs1, nb1 = sb("rs1", [PT, M1]), sb("nb1", [PT, M1])
        rs2, nb2 = sb("rs2", [PT, M2]), sb("nb2", [PT, M2])
        a3 = sb("a3", [PT, M3])
        bias2 = sb("bias2", [PT, M2])
        bias3 = sb("bias3", [PT, M3])
        fin_tmp = squares_sb[:, 0:4 * KT].rearrange("p (i k) -> p i k", i=4)
        fin_h = sb("fin_h", [PT, 3, M3])
        fin_sum = sb("fin_sum", [PT, 4])
        fin_part = sb("fin_part", [PT, 3])
        fin_c = sb("fin_c", [PT, 3])
        xa = sb("xa", [PT, TILES])
        z1, z2, z3, z4 = (sb(f"z{n}", [PT, TILES]) for n in range(1, 5))
        zT = squares_sb[0:TILES, 4 * KT:4 * KT + PT]

        at = [0]

        def take(n):
            at[0] += n
            return vec_sb[:, at[0] - n:at[0]]

        alpha = take(3 * KT).rearrange("p (k i) -> p k i", i=3)
        b0, b1x, b2x = take(KT), take(KT), take(KT)
        gy, by, wy = take(KT), take(KT), take(KT)
        b1, g1, e1 = take(M1), take(M1), take(M1)
        b2, g2, e2 = take(M2), take(M2), take(M2)
        b3, g3, e3, w_h = take(M3), take(M3), take(M3), take(M3)
        bf = take(1)

        tp = [pb(f"tp{i}", [PT, NB]) for i in range(2)]
        acc = [pb(f"acc{i}", [PT, NB]) for i in range(2)]
        yb = [pb(f"yb{i}", [PT, NB]) for i in range(2)]
        turned = pb("turned", [PT, NB])
        tiny = pb("tiny", [PT, NB])
        banks = [*acc, *yb]
        SUM_W, SUM_X, DOT, FIN, HD = 4, 8, 16, 44, 64

        s_vec = sem("s_vec")
        s_raw = sem("s_raw")
        s_w1 = [sem(f"s_w1_{j}") for j in range(-(-KT // SHIFT))]
        s_w2 = sem("s_w2")
        s_w3 = sem("s_w3")
        s_ones = sem("s_ones")
        s_dve = sem("s_dve")
        s_row = sem("s_row")
        s_set = sem("s_set")
        s_index = sem("s_index")
        s_slot = sem("s_slot")
        s_started = sem("s_started")
        s_moving = sem("s_moving")
        s_pad = sem("s_pad")
        s_gath = [sem(f"s_gath{s}") for s in range(SLOTS)]
        s_num = [sem(f"s_num{s}") for s in range(SLOTS)]
        s_spill = [sem(f"s_spill{s}") for s in range(SLOTS)]
        s_wask = sem("s_wask")
        s_wsum = sem("s_wsum")
        s_ask = sem("s_ask")
        s_sum = sem("s_sum")
        s_bb = sem("s_bb")
        s_bps = sem("s_bps")
        s_bpart = sem("s_bpart")
        s_shift2 = sem("s_shift2")
        s_w2g = sem("s_w2g")
        s_w2s = sem("s_w2s")
        s_w2h = sem("s_w2h")
        s_w2l = sem("s_w2l")
        s_w1s = sem("s_w1s")
        s_w1h = sem("s_w1h")
        s_w1l = sem("s_w1l")
        s_scale = sem("s_scale")
        s_tp = sem("s_tp")
        s_hi = sem("s_hi")
        s_lo = sem("s_lo")
        s_dots = sem("s_dots")
        s_rownum = sem("s_rownum")
        s_qt = sem("s_qt")
        s_px = sem("s_px")
        s_rps = sem("s_rps")
        s_rpart = sem("s_rpart")
        s_y = sem("s_y")
        s_ystat = sem("s_ystat")
        s_acc = sem("s_acc")
        s_h1 = sem("s_h1")
        s_bn1 = sem("s_bn1")
        s_h1out = [sem(f"s_h1out{p}") for p in range(2)]
        s_var = sem("s_var")
        s_root = sem("s_root")
        s_ay = sem("s_ay")
        s_afull = sem("s_afull")
        s_arow = sem("s_arow")
        s_h1in = [sem(f"s_h1in{j}") for j in range(N2)]
        s_n1 = sem("s_n1")
        s_n1h = sem("s_n1h")
        s_n1l = sem("s_n1l")
        s_acc2 = sem("s_acc2")
        s_h2 = sem("s_h2")
        s_w3g = sem("s_w3g")
        s_w3m = sem("s_w3m")
        s_w3b = sem("s_w3b")
        s_w3s = sem("s_w3s")
        s_w3h = sem("s_w3h")
        s_w3l = sem("s_w3l")
        s_shift3 = sem("s_shift3")
        s_bias3 = sem("s_bias3")
        s_n2 = sem("s_n2")
        s_n2h = sem("s_n2h")
        s_n2l = sem("s_n2l")
        s_acc3 = sem("s_acc3")
        s_h3 = sem("s_h3")
        s_xin = [sem(f"s_xin{s}") for s in range(XSLOTS)]
        s_xa = sem("s_xa")
        s_fin_in = sem("s_fin_in")
        s_a3 = sem("s_a3")
        s_fin_ps = sem("s_fin_ps")
        s_z = sem("s_z")
        s_sig = sem("s_sig")
        s_zT = sem("s_zT")
        s_zo = sem("s_zo")
        s_out = sem("s_out")

        block = ctx.enter_context(nc.Block())

        ROWS_AT = KT
        Y_AT = {34 + 3 * g: g for g in range(YBANKS)}
        SUM_AT = {78: 0, 110: 1}
        SQUARES_AHEAD_OF = {3: 0, 5: 1}
        TURN_AT = {84 + 32 * j + 3 * g: (j, g) for j in range(2) for g in range(GROUPS)}

        def turns_between(first, last):
            return [TURN_AT[t] for t in range(first, last) if t in TURN_AT]

        def width(g):
            return min(GK, KT - GK * g)

        def h1_block(j, k):
            return h1s[:, :, k, :] if j == 0 else h1r[(j - 1) % 2][:, :, k, :]

        @block.sync
        def _(sp):
            sp.dma_start(raw[:, :, :], cat).then_inc(s_raw, 16)
            sp.dma_start(vec_sb[:, :], vec).then_inc(s_vec, 16)
            sp.dma_start(const_sb[:, :], const).then_inc(s_vec, 16)
            sp.dma_start(w2_raw[:, :, :], w2t).then_inc(s_w2, 16)
            for j in range(-(-KT // SHIFT)):
                k = slice(j * SHIFT, min(KT, (j + 1) * SHIFT))
                sp.dma_start(w1_raw[:, k, :], w1t[:, k, :]).then_inc(s_w1[j], 16)
            for s in range(SLOTS):
                sp.sem_inc(s_spill[s], 16)
            for p in range(2):
                sp.sem_inc(s_h1out[p], 16)

            def numerical(i, s):
                sp.wait_ge(s_y, YBANKS * (2 * i + s // 2 + 1))
                sp.wait_ge(s_spill[s], 16 * i + 16)
                sp.sem_inc(s_moving, 1)
                sp.dma_start(nat[:, s, NT * E:D], num[ds((i * SLOTS + s) * PT, PT), :]).then_inc(s_num[s], 16)

            def spill(i, s):
                sp.wait_ge(s_gath[s], 16 * NT * (i + 1))
                sp.sem_inc(s_moving, 1)
                sp.dma_start(x_spill[ds((i * SLOTS + s) * PT, PT), :], nat[:, s, 0:NT * E]).then_inc(s_spill[s], 16)

            def h1_out(c, p):
                sp.wait_ge(s_h1, 2 + M1 * (c + 1))
                sp.sem_inc(s_moving, 1)
                sp.dma_start(h1_spill[ds(c, 1), :, :].rearrange("o p n -> (o p) n"),
                             h1s[:, p, :, :].rearrange("p m c -> p (m c)")).then_inc(s_h1out[p], 16)

            sp.wait_ge(s_pad, 2)
            for s in range(SLOTS):
                numerical(0, s)
            for s in range(SLOTS):
                spill(0, s)
            with sp.Fori(0, PAIRS - 1) as i:
                numerical(i + 1, 0)
                numerical(i + 1, 1)
                h1_out(2 * i, 0)
                numerical(i + 1, 2)
                numerical(i + 1, 3)
                spill(i + 1, 0)
                spill(i + 1, 1)
                h1_out(2 * i + 1, 1)
                spill(i + 1, 2)
                spill(i + 1, 3)

            def x_in(t):
                s = t % XSLOTS
                if t < XSLOTS:
                    sp.wait_ge(s_y, YBANKS * (2 + CHUNKS))
                    for q in range(SLOTS):
                        sp.wait_ge(s_spill[q], 16 + 16 * TILES // SLOTS)
                else:
                    sp.wait_ge(s_xa, t - XSLOTS + 1)
                rows_t = slice(t * PT, (t + 1) * PT)
                sp.dma_start(nat[:, s, 0:NT * E], x_spill[rows_t, :]).then_inc(s_xin[s], 16)
                sp.dma_start(nat[:, s, NT * E:D], num[rows_t, :]).then_inc(s_xin[s], 16)

            def h1_in(j):
                for b in range(CB):
                    sp.dma_start(h1r[(j - 1) % 2][:, b, :, :].rearrange("p m c -> p (m c)"),
                                 h1_spill[ORDER[j] * CB + b, :, :]).then_inc(s_h1in[j], 16)

            for t in range(XSLOTS):
                x_in(t)
            sp.wait_ge(s_acc, M1 * (2 + CHUNKS))
            for p in range(2):
                sp.wait_ge(s_h1out[p], 16 + 16 * (PAIRS - 1))
            h1_in(1)
            h1_in(2)
            sp.dma_start(w3_raw[:, :, :], w3t).then_inc(s_w3, 16)
            for t in range(XSLOTS, XSLOTS + 4):
                x_in(t)
            sp.wait_ge(s_n1l, M1 * 2)
            h1_in(3)
            for t in range(XSLOTS + 4, TILES):
                x_in(t)
            sp.wait_ge(s_zo, 1)
            sp.dma_start(out.rearrange("(t p) o -> t (p o)", p=PT), zT[:, :]).then_inc(s_out, 16)
            sp.wait_ge(s_out, 16)

        @block.gpsimd
        def _(pool):
            nc.gpsimd.memset(nat[:, 0:SLOTS - 1, NT * E:DP], 0.0).then_inc(s_pad, 1)
            nc.gpsimd.memset(nat[:, SLOTS - 1, NT * E:DP], 0.0).then_inc(s_pad, 1)
            pool.wait_ge(s_index, 1)
            with pool.Fori(0, TILES // SLOTS) as i:
                for s in range(SLOTS):
                    pool.wait_ge(s_y, YBANKS * (2 * i + s // 2 + 1))
                    pool.wait_ge(s_spill[s], 16 * i + 16)
                    nc.gpsimd.tensor_copy(index_slot[:, s, :],
                                          index[:, ds(i * SLOTS + s, 1), :].rearrange("p a f -> p (a f)")
                                          ).then_inc(s_slot, 1)
                    pool.wait_ge(s_slot, SLOTS * i + s + 1)
                    pool.sem_inc(s_started, 1)
                    for f in range(NT):
                        nc.gpsimd.indirect_dma_start(
                            nat[:, s, f * E:(f + 1) * E], None, table_rows,
                            bass.IndirectOffsetOnAxis(ap=index_slot[:, s, f:f + 1], axis=0),
                        ).then_inc(s_gath[s], 16)

            def lower1(j):
                if j >= 2:
                    pool.wait_ge(s_acc2, M2 * (j - 1))
                for k in range(M1):
                    pool.wait_ge(s_n1h, M1 * j + k + 1)
                    nc.gpsimd.tensor_tensor(n1[j % 2][:, 1, k, :].rearrange("p (b c) -> p b c", b=CB), h1_block(j, k),
                                            n1[j % 2][:, 0, k, :].rearrange("p (b c) -> p b c", b=CB),
                                            ALU.subtract).then_inc(s_n1l, 1)

            lower1(0)
            lower1(1)
            pool.wait_ge(s_w3m, 1)
            nc.gpsimd.partition_all_reduce(bound[:, :], mx[:, 3:4], PT, bass.bass_isa.ReduceOp.max).then_inc(s_w3b, 1)
            lower1(2)
            lower1(3)
            for j in range(N2):
                r = slice(ORDER[j] * NB, (ORDER[j] + 1) * NB)
                for k in range(M2):
                    pool.wait_ge(s_n2h, M2 * j + k + 1)
                    nc.gpsimd.tensor_tensor(n2[:, 1, k, r], h2T[:, k, r], n2[:, 0, k, r],
                                            ALU.subtract).then_inc(s_n2l, 1)

        @block.scalar
        def _(act):
            act.sem_inc(s_h1, 2)

            def upper(c, p, j, g):
                if g == 0:
                    act.wait_ge(s_scale, 2 * c + j + 1)
                    if j == 0:
                        act.wait_ge(s_acc, M1 * (c + 1))
                act.wait_ge(s_tp, GROUPS * (SLOTS + 2 * c + j) + g + 1)
                n = width(g)
                nc.scalar.activation(xT[:, p, 0, GK * g:GK * g + n, j * PT:(j + 1) * PT],
                                     tp[(j + g) % 2][:, 0:n * PT].rearrange("p (k r) -> p k r", k=n),
                                     ACT.Copy, scale=sc_x[:, p, j:j + 1]).then_inc(s_hi, 1)

            def relu_h1(c, p, m):
                act.wait_ge(s_acc, M1 * (c + 2) + m + 1)
                if m == 0:
                    act.wait_ge(s_h1out[p], 16 * (c // 2) + 16 if isinstance(c, int) else (c - p) * 8 + 16)
                    act.wait_ge(s_bn1, c + 1)
                for j in range(2):
                    r = slice(j * PT, (j + 1) * PT)
                    last = nc.scalar.activation(h1s[:, p, m, r], acc[m % 2][:, r], ACT.Relu,
                                                bias=b1[:, m:m + 1], scale=iv_h[:, p, j:j + 1])
                last.then_inc(s_h1, 1)

            def sum_squares(s, j, i):
                act.wait_ge(s_gath[s], 16 * NT * (i + 1))
                act.wait_ge(s_num[s], 16 * (i + 1))
                nc.scalar.activation(squares[:, :], nat[:, s, 0:D], ACT.Square,
                                     accum_out=mx[:, j:j + 1]).then_inc(s_ask, 1)

            def times_p(c, p, i):
                act.wait_ge(s_rownum, c + 1)
                for j in range(2):
                    s = 2 * p + j
                    act.wait_ge(s_spill[s], 16 * i + 32)
                    nc.scalar.activation(nat[:, s, 0:D], nat[:, s, 0:D], ACT.Copy,
                                         scale=p_row[:, p, j:j + 1]).then_inc(s_px, 1)

            def chunk(c, p, i, i_next):
                times_p(c, p, i)
                for m in range(M1):
                    if i_next is not None:
                        for j, g in turns_between(KT * m, KT * (m + 1)):
                            upper(c + 1, 1 - p, j, g)
                        if m in SQUARES_AHEAD_OF:
                            j = SQUARES_AHEAD_OF[m]
                            sum_squares(2 * (1 - p) + j, j, i_next)
                    relu_h1(c, p, m)

            def root(n, k):
                act.wait_ge(s_var, n)
                nc.scalar.activation(bn_tmp[:, 1, 0:k], bn_tmp[:, 0, 0:k], ACT.Sqrt).then_inc(s_root, 1)

            act.wait_ge(s_vec, 32)
            act.wait_ge(s_shift2, 1)
            for k in range(M1):
                nc.scalar.activation(w2_raw[:, k, :], w2_raw[:, k, :], ACT.Copy,
                                     scale=g1[:, k:k + 1]).then_inc(s_w2g, 1)
            act.wait_ge(s_w2s, 1)
            nc.scalar.activation(w2[:, 0, :, :], w2_raw[:, :, :], ACT.Copy, scale=sc_w2[:, 0:1]).then_inc(s_w2h, 1)
            act.wait_ge(s_w2l, 1)
            act.wait_ge(s_w1s, 1)
            for k in range(2):
                nc.scalar.activation(w1[:, k, 0, :], w1_raw[:, k, :], ACT.Copy,
                                     scale=sc_w1[:, 0:1]).then_inc(s_w1h, 1)
            sum_squares(0, 0, 0)
            for g in range(GROUPS):
                upper(0, 0, 0, g)
            for k in range(2, KT):
                if k >= SHIFT:
                    act.wait_ge(s_w1l, k - SHIFT + 1)
                nc.scalar.activation(w1[:, k, 0, :], w1_raw[:, k, :], ACT.Copy,
                                     scale=sc_w1[:, 0:1]).then_inc(s_w1h, 1)
            sum_squares(1, 1, 0)
            for g in range(GROUPS):
                upper(0, 0, 1, g)
            with act.Fori(0, PAIRS - 1) as i:
                chunk(2 * i, 0, i, i)
                chunk(2 * i + 1, 1, i, i + 1)
            chunk(CHUNKS - 2, 0, PAIRS - 1, PAIRS - 1)
            times_p(CHUNKS - 1, 1, PAIRS - 1)
            for m in range(M1):
                relu_h1(CHUNKS - 1, 1, m)
                if m == 5:
                    root(1, KT)
            root(2, M1)
            act.wait_ge(s_spill[SLOTS - 1], 16 + 16 * TILES // SLOTS)
            for g in range(GROUPS):
                act.wait_ge(s_afull, g + 1)
                nc.scalar.copy(a_row[:, GK * g * PT:(GK * g + width(g)) * PT],
                               tp[g % 2][:, 0:width(g) * PT]).then_inc(s_arow, 1)

            def upper1(j):
                if j >= 2:
                    act.wait_ge(s_acc2, M2 * (j - 1))
                for k in range(M1):
                    act.wait_ge(s_n1, M1 * j + k + 1)
                    nc.scalar.copy(n1[j % 2][:, 0, k, :].rearrange("p (b c) -> p b c", b=CB),
                                   h1_block(j, k)).then_inc(s_n1h, 1)

            def relu_h2(j):
                for m in range(M2):
                    act.wait_ge(s_acc2, M2 * j + m + 1)
                    nc.scalar.activation(h2T[:, m, ORDER[j] * NB:(ORDER[j] + 1) * NB], banks[m][:, :], ACT.Relu,
                                         bias=bias2[:, m:m + 1], scale=iv_w2[:, 0:1]).then_inc(s_h2, 1)

            act.sem_inc(s_h2, M2)
            upper1(0)
            upper1(1)
            relu_h2(0)
            act.wait_ge(s_w3, 16)
            for k in range(M2):
                nc.scalar.activation(w3_g[:, k, :], w3_raw[:, k, :], ACT.Copy,
                                     scale=g2[:, k:k + 1]).then_inc(s_w3g, 1)
            upper1(2)
            relu_h2(1)
            upper1(3)
            relu_h2(2)
            act.wait_ge(s_w3s, 1)
            nc.scalar.activation(w3[:, 0, :, :], w3_g[:, :, :], ACT.Copy, scale=sc_w3[:, 0:1]).then_inc(s_w3h, 1)
            relu_h2(3)
            root(3, M2)

            def upper2(j):
                r = slice(ORDER[j] * NB, (ORDER[j] + 1) * NB)
                for k in range(M2):
                    act.wait_ge(s_n2, M2 * j + k + 1)
                    nc.scalar.copy(n2[:, 0, k, r], h2T[:, k, r]).then_inc(s_n2h, 1)

            def out_h3(j):
                for m in range(M3):
                    act.wait_ge(s_acc3, M3 * j + m + 1)
                    nc.scalar.activation(h3T[:, m, ORDER[j] * NB:(ORDER[j] + 1) * NB],
                                         banks[(M3 * j + m) % len(banks)][:, :], ACT.Identity,
                                         bias=bias3[:, m:m + 1], scale=iv_w3[:, 0:1]).then_inc(s_h3, 1)

            act.sem_inc(s_h3, len(banks))
            upper2(0)
            upper2(1)
            act.wait_ge(s_bias3, 1)
            for j in range(N2):
                out_h3(j)
                if j + 2 < N2:
                    upper2(j + 2)
            root(4, M3)
            act.wait_ge(s_z, 1)
            nc.scalar.activation(z1[:, :], z4[:, :], ACT.Sigmoid).then_inc(s_sig, 1)
            act.wait_ge(s_zT, 1)
            nc.scalar.copy(zT[:, :], turned[0:TILES, 0:PT]).then_inc(s_zo, 1)

        @block.vector
        def _(dve):
            v = nc.vector
            done = [0]

            def link(ins):
                done[0] += 1
                ins.then_inc(s_dve, 1)
                dve.wait_ge(s_dve, done[0])

            def largest(out, in_, axis=AX.X):
                return v.tensor_reduce(out, in_, axis, ALU.max, apply_absolute_value=True)

            def scale_of(linked, col, squared=False):
                linked(v.tensor_scalar(bound[:, :], col, TINY, None, ALU.max))
                bits = bound[:, :].bitcast(i32)
                if squared:
                    linked(v.tensor_scalar(power[:, :], bits, EXPONENT, 1, ALU.bitwise_and, ALU.logical_shift_right))
                    linked(v.tensor_scalar(power[:, :], power[:, :], float(BIAS), None, ALU.add))
                    bits = power[:, :]
                linked(v.tensor_scalar(power[:, :], bits, EXPONENT, None, ALU.bitwise_and))
                linked(v.reciprocal(rpower[:, :], power[:, :].bitcast(f32)))

            def three_parts(linked, part, rest, val):
                linked(v.tensor_copy(part[:, :, :, 0], val))
                linked(v.tensor_tensor(rest, val, part[:, :, :, 0], ALU.subtract))
                linked(v.tensor_copy(part[:, :, :, 1], rest))
                linked(v.tensor_tensor(part[:, :, :, 2], rest, part[:, :, :, 1], ALU.subtract))
                linked(v.tensor_copy(part[:, :, :, 3:5], part[:, :, :, 0:2]))
                linked(v.tensor_copy(part[:, :, :, 5], part[:, :, :, 0]))

            def weight_scale(col, sc, iv, factor):
                scale_of(link, col)
                link(v.tensor_scalar(sc[:, :], rpower[:, :], 2.0 ** ROOM, None, ALU.mult))
                link(v.tensor_scalar(iv[:, :], power[:, :].bitcast(f32), factor * 2.0 ** -ROOM, None, ALU.mult))

            dve.sem_inc(s_bn1, 2)
            dve.sem_inc(s_lo, 2)
            dve.sem_inc(s_ystat, 2)
            dve.wait_ge(s_raw, 16)
            dve.wait_ge(s_vec, 32)
            link(v.tensor_copy(ixf[:, :, :], raw[:, :, :]))
            link(v.tensor_scalar(wrap_f[:, :, :], ixf[:, :, :], 0.0, float(V), ALU.is_lt, ALU.mult))
            link(v.tensor_tensor(ixf[:, :, :], ixf[:, :, :], wrap_f[:, :, :], ALU.add))
            link(v.tensor_scalar(ixf[:, :, :], ixf[:, :, :], 0.0, float(V - 1), ALU.max, ALU.min))
            v.tensor_tensor(index[:, :, :], ixf[:, :, :],
                            table_base.unsqueeze(1).broadcast_to([PT, TILES, NT]), ALU.add).then_inc(s_index, 1)
            v.memset(ones[:, :], 1.0).then_inc(s_ones, 1)
            link(v.tensor_tensor(cc_tmp[:, 0, :], b0, alpha[:, :, 1], ALU.mult))
            link(v.tensor_tensor(cc_tmp[:, 1, :], b0, alpha[:, :, 2], ALU.mult))
            link(v.tensor_tensor(cc_tmp[:, 2, :], b1x, alpha[:, :, 2], ALU.mult))
            v.reduce_sum(part1[:, 0:3], cc_tmp[:, :, :], axis=AX.X)
            largest(part1[:, 3:4], vec_sb[:, 0:3 * KT]).then_inc(s_wask, 1)
            dve.wait_ge(s_wsum, 1)
            link(v.tensor_copy(cc[:, :], tiny[:, 0:3]))
            weight_scale(tiny[:, 3:4], sc_al, iv_al, 1.0)
            link(v.tensor_scalar(al[:, :, 0, :], alpha, sc_al[:, 0:1], None, ALU.mult))
            link(v.scalar_tensor_tensor(out=al[:, :, 1, :], in0=alpha, scalar=sc_al[:, 0:1], in1=al[:, :, 0, :],
                                        op0=ALU.mult, op1=ALU.subtract))
            link(v.tensor_copy(bb[:, :, 0], b0))
            link(v.tensor_copy(bb[:, :, 1], b1x))
            b_terms = bb_part[:, :, :].rearrange("p k (b i) -> p k b i", i=TERMS)
            link(v.tensor_copy(b_terms[:, :, :, 0], bb[:, :, :]))
            link(v.tensor_tensor(bb_rest[:, :, :], bb[:, :, :], b_terms[:, :, :, 0], ALU.subtract))
            link(v.tensor_copy(b_terms[:, :, :, 3], bb_rest[:, :, :]))
            link(v.tensor_tensor(b_terms[:, :, :, 5], bb_rest[:, :, :], b_terms[:, :, :, 3], ALU.subtract))
            link(v.tensor_copy(b_terms[:, :, :, 1], b_terms[:, :, :, 0]))
            link(v.tensor_copy(b_terms[:, :, :, 2], b_terms[:, :, :, 0]))
            link(v.tensor_copy(b_terms[:, :, :, 4], b_terms[:, :, :, 3]))
            v.tensor_copy(ident16[:, :], ident).then_inc(s_bb, 1)
            v.memset(r_part[:, :, :], 0.0)
            link(v.memset(b_part[:, :], 0.0))
            for n, bank in enumerate([*yb, *acc, tp[0]]):
                k = min(GK, KT - GK * n)
                dve.wait_ge(s_bps, n + 1)
                v.tensor_copy(b_part[0:2 * TERMS, GK * n * PT:(GK * n + k) * PT],
                              bank[0:2 * TERMS, 0:k * PT]).then_inc(s_bpart, 1)
            dve.wait_ge(s_shift2, 1)
            link(v.tensor_tensor(bias2[:, :], turned[:, 0:M2], b2, ALU.add))
            dve.wait_ge(s_w2g, M1)
            largest(mx[:, 2:3], w2_raw[:, :, :].rearrange("p k m -> p (k m)")).then_inc(s_wask, 1)
            dve.wait_ge(s_wsum, 2)
            weight_scale(tiny[:, SUM_W:SUM_W + 1], sc_w2, iv_w2, 1.0 / NSCALE)
            dve.sem_inc(s_w2s, 1)
            dve.wait_ge(s_w2h, 1)
            v.scalar_tensor_tensor(out=w2[:, 1, :, :].rearrange("p k m -> p (k m)"),
                                   in0=w2_raw[:, :, :].rearrange("p k m -> p (k m)"), scalar=sc_w2[:, 0:1],
                                   in1=w2[:, 0, :, :].rearrange("p k m -> p (k m)"),
                                   op0=ALU.mult, op1=ALU.subtract).then_inc(s_w2l, 1)
            for j in range(len(s_w1)):
                dve.wait_ge(s_w1[j], 16)
                k = slice(j * SHIFT, min(KT, (j + 1) * SHIFT))
                last = largest(mx_w1[:, j:j + 1], w1_raw[:, k, :].rearrange("p k m -> p (k m)"))
            link(last)
            v.reduce_max(mx[:, 2:3], mx_w1[:, 0:len(s_w1)], axis=AX.X).then_inc(s_wask, 1)
            dve.wait_ge(s_wsum, 3)
            weight_scale(tiny[:, SUM_W:SUM_W + 1], sc_w1, iv_w1, 1.0)
            dve.sem_inc(s_w1s, 1)

            SET_LINKS = 6

            def tile_scale(c, p, j):
                t = 2 * c + j
                local = [0]

                def set_link(ins):
                    local[0] += 1
                    ins.then_inc(s_set, 1)
                    dve.wait_ge(s_set, SET_LINKS * t + local[0])

                dve.wait_ge(s_sum, t + 1)
                scale_of(set_link, tiny[:, SUM_X + j:SUM_X + j + 1], squared=True)
                v.tensor_scalar(sc_x[:, p, j:j + 1], rpower[:, :], 2.0 ** ROOM, None, ALU.mult)
                v.tensor_scalar(iv_h[:, p, j:j + 1], power[:, :].bitcast(f32), 2.0 ** -ROOM, iv_w1[:, 0:1],
                                ALU.mult, ALU.mult)
                set_link(v.tensor_scalar(iv_d[:, p, j:j + 1], power[:, :].bitcast(f32), 2.0 ** -ROOM, iv_al[:, 0:1],
                                         ALU.mult, ALU.mult))
                dve.sem_inc(s_scale, 1)

            def lower(c, p, j, g):
                dve.wait_ge(s_hi, GROUPS * (2 * c + j) + g + 1)
                n = width(g)
                part = [xT[:, p, q, GK * g:GK * g + n, j * PT:(j + 1) * PT] for q in range(2)]
                v.scalar_tensor_tensor(out=part[1], in0=tp[(j + g) % 2][:, 0:n * PT].rearrange("p (k r) -> p k r", k=n),
                                       scalar=sc_x[:, p, j:j + 1], in1=part[0],
                                       op0=ALU.mult, op1=ALU.subtract).then_inc(s_lo, 1)

            def lower_w1(k):
                dve.wait_ge(s_w1h, k + 1)
                v.scalar_tensor_tensor(out=w1[:, k, 1, :], in0=w1_raw[:, k, :], scalar=sc_w1[:, 0:1],
                                       in1=w1[:, k, 0, :], op0=ALU.mult, op1=ALU.subtract).then_inc(s_w1l, 1)

            tile_scale(0, 0, 0)
            for k in range(2):
                lower_w1(k)
            for g in range(GROUPS):
                lower(0, 0, 0, g)
            for k in range(2, KT):
                lower_w1(k)
            tile_scale(0, 0, 1)
            for g in range(GROUPS):
                lower(0, 0, 1, g)

            LINKS = 18

            def chunk(c, p, ahead, before_bn1):
                local = [0]

                def row_link(ins):
                    local[0] += 1
                    ins.then_inc(s_row, 1)
                    dve.wait_ge(s_row, LINKS * c + local[0])

                dve.wait_ge(s_dots, c + 1)
                row_link(v.tensor_copy(dot6[:, :, :], tiny[:, DOT:DOT + 16].rearrange("p (j i) -> p j i", i=8)[:, :, 0:6]))
                row_link(v.tensor_tensor(dot3[:, :, :], dot6[:, :, 0:3], dot6[:, :, 3:6], ALU.add))
                row_link(v.tensor_tensor(dot3[:, :, :], dot3[:, :, :],
                                         iv_d[:, p, :].unsqueeze(2).broadcast_to([PT, 2, 3]), ALU.mult))
                row_link(v.tensor_scalar(ra[:, :], dot3[:, :, 0], 1.0, None, ALU.add))
                v.tensor_tensor(r2[:, :], ra[:, :], dot3[:, :, 2], ALU.mult)
                row_link(v.tensor_tensor(r1[:, :], ra[:, :], dot3[:, :, 1], ALU.mult))
                row_link(v.tensor_scalar(rf[:, :], r1[:, :], cc[:, 0:1], 1.0, ALU.add, ALU.add))
                row_link(v.scalar_tensor_tensor(out=r3[:, :], in0=r2[:, :], scalar=cc[:, 1:2], in1=rf[:, :],
                                                op0=ALU.add, op1=ALU.mult))
                row_link(v.tensor_scalar(rt[:, :], r3[:, :], cc[:, 2:3], 1.0, ALU.add, ALU.add))
                v.tensor_scalar(qt_row[:, :, 1], rt[:, :], -1.0, None, ALU.add)
                row_link(v.tensor_tensor(rq[:, :], rf[:, :], rt[:, :], ALU.mult))
                v.tensor_scalar(qt_row[:, :, 0], rq[:, :], -1.0, None, ALU.add)
                row_link(v.tensor_tensor(p_row[:, p, :], ra[:, :], rq[:, :], ALU.mult))
                dve.sem_inc(s_rownum, 1)
                three_parts(row_link, qt_part[:, :, :].rearrange("p j (q i) -> p j q i", i=TERMS),
                            qt_rest[:, :, :], qt_row[:, :, :])
                dve.sem_inc(s_qt, 1)
                v.tensor_copy(rows[:, 0, ds(2 * c, 2)], p_row[:, p, :])
                row_link(v.tensor_copy(rows[:, 1:3, ds(2 * c, 2)], qt_row[:, :, :].rearrange("p j q -> p q j")))
                dve.wait_ge(s_rps, c + 1)
                v.tensor_copy(r_part[0:2 * TERMS, p, :], turned[0:2 * TERMS, 0:C]).then_inc(s_rpart, 1)
                for g in range(YBANKS):
                    dve.wait_ge(s_y, YBANKS * (c + 2) + g + 1)
                    for k in range(min(YK, KT - YK * g)):
                        last = v.bn_stats(y_stats[:, YK * g + k, ds(c * BN, BN)], yb[g % 2][:, k * C:(k + 1) * C])
                    last.then_inc(s_ystat, 1)
                if ahead:
                    for j in range(2):
                        tile_scale(c + 1, 1 - p, j)
                        for g in range(GROUPS):
                            lower(c + 1, 1 - p, j, g)
                before_bn1()
                dve.wait_ge(s_h1, 2 + M1 * (c + 1))
                for m in range(M1):
                    last = v.bn_stats(h1_stats[:, m, ds(c * BN, BN)], h1s[:, p, m, :])
                row_link(last)
                dve.sem_inc(s_bn1, 1)
                assert local[0] == LINKS, local[0]

            def inverse_root(n, var, k):
                t = [bn_tmp[:, j, 0:k] for j in range(5)]
                link(v.tensor_scalar(t[0], var, EPS, None, ALU.add))
                dve.sem_inc(s_var, 1)
                dve.wait_ge(s_root, n)
                link(v.reciprocal(t[2], t[1]))
                link(v.tensor_tensor(t[3], t[2], t[2], ALU.mult))
                link(v.tensor_tensor(t[3], t[3], t[0], ALU.mult))
                link(v.tensor_scalar(t[3], t[3], -0.5, 1.5, ALU.mult, ALU.add))
                link(v.tensor_tensor(t[4], t[2], t[3], ALU.mult))
                return t[4]

            def aggregate(mv, stats, k):
                for j in range(k):
                    last = v.bn_aggr(mv[:, j, :], stats[:, j, :])
                link(last)

            def fold_y():
                dve.wait_ge(s_ystat, 2 + YBANKS * CHUNKS)
                aggregate(mvy, y_stats, KT)
                r = inverse_root(1, mvy[:, :, 1], KT)
                link(v.tensor_tensor(ay[:, :], r, gy, ALU.mult))
                link(v.tensor_tensor(ay[:, :], ay[:, :], wy, ALU.mult))
                dve.sem_inc(s_ay, 1)

            def cross_constants():
                link(v.tensor_tensor(fin_tmp[:, 0, :], b0, ay[:, :], ALU.mult))
                link(v.tensor_tensor(fin_tmp[:, 1, :], b1x, ay[:, :], ALU.mult))
                link(v.tensor_tensor(fin_tmp[:, 3, :], mvy[:, :, 0], b2x, ALU.add))
                link(v.tensor_tensor(fin_tmp[:, 3, :], b2x, fin_tmp[:, 3, :], ALU.subtract))
                link(v.tensor_tensor(fin_tmp[:, 3, :], fin_tmp[:, 3, :], ay[:, :], ALU.mult))
                link(v.tensor_tensor(fin_tmp[:, 2, :], by, wy, ALU.mult))
                link(v.tensor_tensor(fin_tmp[:, 2, :], fin_tmp[:, 2, :], fin_tmp[:, 3, :], ALU.add))
                link(v.reduce_sum(fin_sum[:, 0:3], fin_tmp[:, 0:3, :], axis=AX.X))

            def nothing():
                pass

            with dve.Fori(0, PAIRS - 1) as i:
                chunk(2 * i, 0, True, nothing)
                chunk(2 * i + 1, 1, True, nothing)
            chunk(CHUNKS - 2, 0, True, nothing)
            chunk(CHUNKS - 1, 1, False, fold_y)

            def fold(n, mv, stats, k, rs, nb):
                aggregate(mv, stats, k)
                r = inverse_root(n, mv[:, :, 1], k)
                link(v.tensor_scalar(rs[:, :], r, NSCALE, None, ALU.mult))
                link(v.scalar_tensor_tensor(out=nb[:, :], in0=mv[:, :, 0], scalar=-1.0, in1=rs[:, :],
                                            op0=ALU.mult, op1=ALU.mult))

            def normalise1(j):
                if j:
                    dve.wait_ge(s_h1in[j], 16 * CB)
                for k in range(M1):
                    v.tensor_scalar(h1_block(j, k), h1_block(j, k), rs1[:, k:k + 1], nb1[:, k:k + 1],
                                    ALU.mult, ALU.add).then_inc(s_n1, 1)

            def read_out(t):
                s = t % XSLOTS
                dve.wait_ge(s_xin[s], 32 * (t // XSLOTS + 1))
                v.tensor_tensor_reduce(out=nat[:, s, 0:D], in0=nat[:, s, 0:D], in1=a_row[:, 0:D],
                                       scale=1.0, scalar=0.0, op0=ALU.mult, op1=ALU.add,
                                       accum_out=xa[:, t:t + 1]).then_inc(s_xa, 1)

            fold(2, mv1, h1_stats, M1, rs1, nb1)
            normalise1(0)
            normalise1(1)
            cross_constants()
            dve.wait_ge(s_arow, GROUPS)
            per = TILES // N2
            for j in range(N2):
                for t in range(j * per, (j + 1) * per):
                    read_out(t)
                for m in range(M2):
                    dve.wait_ge(s_h2, M2 * (j + 1) + m + 1)
                    last = v.bn_stats(h2_stats[:, m, j * BN:(j + 1) * BN],
                                      h2T[:, m, ORDER[j] * NB:(ORDER[j] + 1) * NB])
                if j == 0:
                    dve.wait_ge(s_w3g, M2)
                    largest(mx[:, 3:4], w3_g[:, :, :].rearrange("p k m -> p (k m)")).then_inc(s_w3m, 1)
                if j == 1:
                    dve.wait_ge(s_w3b, 1)
                    weight_scale(bound[:, 0:1], sc_w3, iv_w3, 1.0 / NSCALE)
                    dve.sem_inc(s_w3s, 1)
                if j == 2:
                    dve.wait_ge(s_w3h, 1)
                    v.scalar_tensor_tensor(out=w3[:, 1, :, :].rearrange("p k m -> p (k m)"),
                                           in0=w3_g[:, :, :].rearrange("p k m -> p (k m)"), scalar=sc_w3[:, 0:1],
                                           in1=w3[:, 0, :, :].rearrange("p k m -> p (k m)"),
                                           op0=ALU.mult, op1=ALU.subtract).then_inc(s_w3l, 1)
                if j + 2 < N2:
                    normalise1(j + 2)
            link(last)
            fold(3, mv2, h2_stats, M2, rs2, nb2)
            for j in range(N2):
                r = slice(ORDER[j] * NB, (ORDER[j] + 1) * NB)
                for k in range(M2):
                    v.tensor_scalar(h2T[:, k, r], h2T[:, k, r], rs2[:, k:k + 1], nb2[:, k:k + 1],
                                    ALU.mult, ALU.add).then_inc(s_n2, 1)
                if j == 0:
                    dve.wait_ge(s_shift3, 1)
                    link(v.tensor_tensor(bias3[:, :], turned[:, 0:M3], b3, ALU.add))
                    dve.sem_inc(s_bias3, 1)
            for j in range(N2):
                for m in range(M3):
                    dve.wait_ge(s_h3, len(banks) + M3 * j + m + 1)
                    last = v.bn_stats(h3_stats[:, m, j * BN:(j + 1) * BN],
                                      h3T[:, m, ORDER[j] * NB:(ORDER[j] + 1) * NB])
            link(last)
            aggregate(mv3, h3_stats, M3)
            r = inverse_root(4, mv3[:, :, 1], M3)
            link(v.tensor_tensor(a3[:, :], r, g3, ALU.mult))
            link(v.tensor_tensor(a3[:, :], a3[:, :], w_h, ALU.mult))
            dve.sem_inc(s_a3, 1)
            link(v.tensor_tensor(fin_h[:, 0, :], mv3[:, :, 0], a3[:, :], ALU.mult))
            link(v.tensor_tensor(fin_h[:, 1, :], e3, w_h, ALU.mult))
            link(v.tensor_tensor(fin_h[:, 2, :], fin_h[:, 1, :], fin_h[:, 0, :], ALU.subtract))
            link(v.reduce_sum(fin_sum[:, 3:4], fin_h[:, 2, :], axis=AX.X))
            link(v.tensor_copy(fin_part[:, 0:2], fin_sum[:, 0:2]))
            link(v.tensor_tensor(fin_part[:, 2:3], fin_sum[:, 2:3], fin_sum[:, 3:4], ALU.add))
            link(v.tensor_tensor(fin_part[:, 2:3], fin_part[:, 2:3], bf, ALU.add))
            dve.sem_inc(s_fin_in, 1)
            dve.wait_ge(s_fin_ps, 1)
            link(v.tensor_copy(fin_c[:, :], tiny[:, FIN:FIN + 3]))
            link(v.tensor_tensor(z1[:, :], rows[:, 0, :], xa[:, :], ALU.mult))
            link(v.scalar_tensor_tensor(out=z2[:, :], in0=rows[:, 1, :], scalar=fin_c[:, 0:1], in1=z1[:, :],
                                        op0=ALU.mult, op1=ALU.add))
            link(v.scalar_tensor_tensor(out=z3[:, :], in0=rows[:, 2, :], scalar=fin_c[:, 1:2], in1=z2[:, :],
                                        op0=ALU.mult, op1=ALU.add))
            v.scalar_tensor_tensor(out=z4[:, :], in0=tiny[:, HD:HD + TILES], scalar=fin_c[:, 2:3], in1=z3[:, :],
                                   op0=ALU.add, op1=ALU.add).then_inc(s_z, 1)

        @block.tensor
        def _(pe):
            mm = nc.tensor.matmul
            pe.sem_inc(s_tp, GROUPS * SLOTS)
            pe.sem_inc(s_acc, 2 * M1)
            pe.sem_inc(s_y, 2 * YBANKS)

            def total(asked, n, col, numbers, given):
                pe.wait_ge(asked, n)
                w = numbers.shape[1]
                mm(tiny[:, col:col + w], ones[:, :], numbers, start=True, stop=True).then_inc(given, 1)

            def split_mm(out, w, x, first, last):
                mm(out, w(0), x(0), start=first, stop=False)
                mm(out, w(0), x(1), start=False, stop=False)
                return mm(out, w(1), x(0), start=False, stop=last)

            def shift(out, w, e, kt, mt, s_done):
                for m in range(mt):
                    for k in range(kt):
                        last = mm(out[:, m:m + 1], w[:, k, m * PT:(m + 1) * PT], e[:, k:k + 1],
                                  start=(k == 0), stop=(k == kt - 1))
                last.then_inc(s_done, 1)

            def turn(c, p, i, j, g):
                if g == 0:
                    pe.wait_ge(s_gath[2 * p + j], 16 * NT * (i + 1))
                    pe.wait_ge(s_num[2 * p + j], 16 * (i + 1))
                pe.wait_ge(s_lo, GROUPS * (2 * c + j) + g + 1)
                for k in range(width(g)):
                    last = nc.tensor.transpose(tp[(j + g) % 2][:, k * PT:(k + 1) * PT],
                                               nat[:, 2 * p + j, (GK * g + k) * PT:(GK * g + k + 1) * PT], ident)
                last.then_inc(s_tp, 1)

            def dots(c, p):
                pe.wait_ge(s_lo, 2 + 2 * GROUPS * (c + 1))
                for j in range(2):
                    o = DOT + 8 * j
                    for k in range(KT):
                        mm(tiny[:, o:o + 6], xT[:, p, 0, k, j * PT:(j + 1) * PT],
                           al[:, k, :, :].rearrange("p s i -> p (s i)"), start=(k == 0), stop=False)
                        last = mm(tiny[:, o:o + 3], xT[:, p, 1, k, j * PT:(j + 1) * PT], al[:, k, 0, :],
                                  start=False, stop=(k == KT - 1))
                last.then_inc(s_dots, 1)

            def turn_rows(c, p):
                pe.wait_ge(s_qt, c + 1)
                for j in range(2):
                    last = mm(turned[0:2 * TERMS, j * PT:(j + 1) * PT], qt_part[:, j, :], ident16[:, :],
                              start=True, stop=True)
                last.then_inc(s_rps, 1)

            def y_bank(c, p, g):
                if g == 0:
                    pe.wait_ge(s_px, 2 * c + 2)
                    pe.wait_ge(s_rpart, c + 1)
                pe.wait_ge(s_ystat, YBANKS * c + g + 1)
                for k in range(min(YK, KT - YK * g)):
                    f = slice((YK * g + k) * PT, (YK * g + k + 1) * PT)
                    for j in range(2):
                        mm(yb[g % 2][:, k * C + j * PT:k * C + (j + 1) * PT], nat[:, 2 * p + j, f], ident,
                           is_transpose=True, start=(j == 0), stop=False)
                    last = mm(yb[g % 2][:, k * C:(k + 1) * C], b_part[:, f], r_part[:, p, :], start=False, stop=True)
                last.then_inc(s_y, 1)

            def chunk(c, p, i_next):
                dots(c, p)
                for m in range(M1):
                    pe.wait_ge(s_h1, M1 * c + m + 1)
                    for k in range(KT):
                        t = KT * m + k
                        if t == ROWS_AT:
                            turn_rows(c, p)
                        if t in Y_AT:
                            y_bank(c, p, Y_AT[t])
                        if i_next is not None and t in SUM_AT:
                            j = SUM_AT[t]
                            total(s_ask, 2 * (c + 1) + j + 1, SUM_X + j, mx[:, j:j + 1], s_sum)
                        if i_next is not None and t in TURN_AT:
                            turn(c + 1, 1 - p, i_next, *TURN_AT[t])
                        last = split_mm(acc[m % 2][:, 0:C], lambda s: w1[:, k, s, m * PT:(m + 1) * PT],
                                        lambda s: xT[:, p, s, k, :], k == 0, k == KT - 1)
                    last.then_inc(s_acc, 1)

            pe.wait_ge(s_ones, 1)
            total(s_wask, 1, 0, part1[:, :], s_wsum)
            pe.wait_ge(s_bb, 1)
            for n, bank in enumerate([*yb, *acc, tp[0]]):
                for k in range(min(GK, KT - GK * n)):
                    last = mm(bank[0:2 * TERMS, k * PT:(k + 1) * PT], bb_part[:, GK * n + k, :], ident16[:, :],
                              start=True, stop=True)
                last.then_inc(s_bps, 1)
            pe.wait_ge(s_vec, 32)
            pe.wait_ge(s_w2, 16)
            shift(turned, w2_raw, e1, M1, M2, s_shift2)
            total(s_wask, 2, SUM_W, mx[:, 2:3], s_wsum)
            total(s_wask, 3, SUM_W, mx[:, 2:3], s_wsum)
            pe.wait_ge(s_pad, 2)
            pe.wait_ge(s_bpart, 5)
            for j in range(2):
                total(s_ask, j + 1, SUM_X + j, mx[:, j:j + 1], s_sum)
                for g in range(GROUPS):
                    turn(0, 0, 0, j, g)
            pe.wait_ge(s_w1l, KT)
            with pe.Fori(0, PAIRS - 1) as i:
                chunk(2 * i, 0, i)
                chunk(2 * i + 1, 1, i + 1)
            chunk(CHUNKS - 2, 0, PAIRS - 1)
            chunk(CHUNKS - 1, 1, None)

            pe.wait_ge(s_ay, 1)
            for g in range(GROUPS):
                if g >= 2:
                    pe.wait_ge(s_arow, g - 1)
                for k in range(width(g)):
                    last = mm(tp[g % 2][:, k * PT:(k + 1) * PT], ay[:, GK * g + k:GK * g + k + 1].broadcast_to([PT, PT]),
                              ident, start=True, stop=True)
                last.then_inc(s_afull, 1)

            pe.wait_ge(s_w2l, 1)
            with pe.Fori(0, N2 // 2) as i:
                for b in range(2):
                    for k in range(M1):
                        pe.wait_ge(s_n1l, 2 * M1 * i + M1 * b + k + 1)
                        for m in range(M2):
                            if k == 0:
                                pe.wait_ge(s_h2, 2 * M2 * i + M2 * b + m + 1)
                            last = split_mm(banks[m][:, :], lambda s: w2[:, s, k, m * PT:(m + 1) * PT],
                                            lambda s: n1[b][:, s, k, :], k == 0, k == M1 - 1)
                            if k == M1 - 1:
                                last.then_inc(s_acc2, 1)
            pe.wait_ge(s_w3, 16)
            shift(turned, w3_raw, e2, M2, M3, s_shift3)
            pe.wait_ge(s_w3l, 1)
            for j in range(N2):
                r = slice(ORDER[j] * NB, (ORDER[j] + 1) * NB)
                for k in range(M2):
                    pe.wait_ge(s_n2l, M2 * j + k + 1)
                    for m in range(M3):
                        if k == 0:
                            pe.wait_ge(s_h3, M3 * j + m + 1)
                        last = split_mm(banks[(M3 * j + m) % len(banks)][:, :],
                                        lambda s: w3[:, s, k, m * PT:(m + 1) * PT],
                                        lambda s: n2[:, s, k, r], k == 0, k == M2 - 1)
                        if k == M2 - 1:
                            last.then_inc(s_acc3, 1)
            pe.wait_ge(s_a3, 1)
            for t in range(TILES):
                for m in range(M3):
                    mm(tiny[:, HD + t:HD + t + 1], h3T[:, m, t * PT:(t + 1) * PT], a3[:, m:m + 1],
                       start=(m == 0), stop=(m == M3 - 1))
            pe.wait_ge(s_fin_in, 1)
            mm(tiny[:, FIN:FIN + 3], ones[:, :], fin_part[:, :], start=True, stop=True).then_inc(s_fin_ps, 1)
            pe.wait_ge(s_sig, 1)
            nc.tensor.transpose(turned[0:TILES, 0:PT], z1[:, :], ident).then_inc(s_zT, 1)


def kernel(r_numerical_input, r_categorical_input, L0_rec_emb_tables, L0_rec_cross_alphas, L0_rec_cross_bias,
           L0_rec_w1, L0_rec_b1, L0_rec_g1, L0_rec_be1, L0_rec_w2, L0_rec_b2, L0_rec_g2, L0_rec_be2,
           L0_rec_w3, L0_rec_b3, L0_rec_bn_g, L0_rec_bn_b, L0_rec_wf, L0_rec_bf):
    import numpy as np
    import concourse.bacc as bacc
    from concourse import mybir
    from concourse.bass_utils import run_bass_kernel_spmd

    P = 128

    def columns(v):
        v = np.asarray(v).reshape(-1)
        n = -(-v.shape[0] // P)
        full = np.zeros((n * P,), v.dtype)
        full[:v.shape[0]] = v
        return full.reshape(n, P).T

    def weights(w):
        w = np.asarray(w)
        kt = -(-w.shape[1] // P)
        full = np.zeros((kt * P, w.shape[0]), w.dtype)
        full[:w.shape[1]] = w.T
        return np.ascontiguousarray(full.reshape(kt, P, w.shape[0]).transpose(1, 0, 2))

    cat = np.asarray(r_categorical_input)
    tables = np.ascontiguousarray(L0_rec_emb_tables)
    nt, v_rows, e = tables.shape
    d = L0_rec_w1.shape[1]
    alphas = np.stack([columns(a) for a in np.asarray(L0_rec_cross_alphas)], axis=2).reshape(P, -1)
    bias = [columns(b) for b in np.asarray(L0_rec_cross_bias)]
    bn_g, bn_b, wf = (np.asarray(a).reshape(-1) for a in (L0_rec_bn_g, L0_rec_bn_b, L0_rec_wf))
    vec = [alphas, *bias, columns(bn_g[:d]), columns(bn_b[:d]), columns(wf[:d]),
           columns(L0_rec_b1), columns(L0_rec_g1), columns(L0_rec_be1),
           columns(L0_rec_b2), columns(L0_rec_g2), columns(L0_rec_be2),
           columns(L0_rec_b3), columns(bn_g[d:]), columns(bn_b[d:]), columns(wf[d:]), columns(L0_rec_bf)]
    base = np.broadcast_to(np.arange(nt, dtype=np.float32) * v_rows, (P, nt))
    arrays = {
        "cat": np.ascontiguousarray(cat.reshape(-1, P, nt).transpose(1, 0, 2)),
        "num": np.ascontiguousarray(r_numerical_input),
        "table": tables,
        "vec": np.ascontiguousarray(np.concatenate(vec, axis=1)),
        "const": np.ascontiguousarray(np.concatenate([np.eye(P, dtype=np.float32), base], axis=1)),
        "w1t": weights(L0_rec_w1), "w2t": weights(L0_rec_w2), "w3t": weights(L0_rec_w3),
    }
    nc = bacc.Bacc("TRN2", target_bir_lowering=False, num_devices=1)
    args = [nc.dram_tensor(name, a.shape, mybir.dt.from_np(a.dtype), kind="ExternalInput").ap()
            for name, a in arrays.items()]
    out = nc.dram_tensor("out", (cat.shape[0], 1), mybir.dt.float32, kind="ExternalOutput").ap()
    wide_cross_mlp(nc, *args, out)
    return run_bass_kernel_spmd(nc, [arrays], core_ids=[0]).results[0]["out"]
```

```python
def wide_cross_mlp(nc, cat, num, table, vec, const, w1t, w2t, w3t, out):
    from contextlib import ExitStack

    import concourse.bass as bass
    from concourse import mybir

    f32, f16, bf16, i32 = mybir.dt.float32, mybir.dt.float16, mybir.dt.bfloat16, mybir.dt.int32
    ALU = mybir.AluOpType
    ACT = mybir.ActivationFunctionType
    AX = mybir.AxisListType
    ds = bass.ds

    PT = 128
    NT, V, E = table.shape
    B, NUM = num.shape
    D = NT * E + NUM
    TILES = B // PT
    C = 2 * PT
    CHUNKS = B // C
    PAIRS = CHUNKS // 2
    KT = -(-D // PT)
    DP = KT * PT
    LAST = D - (KT - 1) * PT
    TWIN = PT // 2
    assert LAST <= TWIN
    L1, L2, L3 = w1t.shape[2], w2t.shape[2], w3t.shape[2]
    M1, M2, M3 = L1 // PT, L2 // PT, L3 // PT
    NB = 512
    N2 = B // NB
    CB = NB // C
    GK = NB // PT
    GROUPS = -(-KT // GK)
    YK = NB // C
    YBLOCKS = -(-KT // YK)
    SLOTS = 4
    XSLOTS = 3
    SHIFT = 4
    BN = 6
    EPS = 1e-05
    ROOM = 14
    NSCALE = 512.0
    TINY = 2.0 ** -100
    BIAS = 127 << 22
    EXPONENT = 0x7F800000
    ORDER = [N2 - 1] + list(range(N2 - 1))
    assert CB == 2 and NSCALE * B ** 0.5 < 2.0 ** 15
    table_rows = table.rearrange("a b c -> (a b) c")

    x_spill = nc.dram_tensor("x_spill", (B, NT * E), f32).ap()
    h1_spill = nc.dram_tensor("h1_spill", (CHUNKS - CB, PT, M1 * C), f32).ap()

    ctx = ExitStack()
    with ctx:
        def sb(name, shape, dt=f32):
            return ctx.enter_context(nc.sbuf_tensor(name, shape, dt))

        def pb(name, shape):
            return ctx.enter_context(nc.psum_tensor(name, shape, f32))

        def sem(name):
            return ctx.enter_context(nc.semaphore(name))

        W1_WORDS = KT * L1
        STAGE = 2 * M1 * C
        arena = sb("arena", [PT, W1_WORDS + STAGE])
        w1 = arena[:, 0:W1_WORDS].bitcast(f16).rearrange("p (k s m) -> p k s m", k=KT, s=2)
        w1_raw = arena[:, SHIFT * L1:(SHIFT + KT) * L1].rearrange("p (k m) -> p k m", k=KT)
        h1s = arena[:, W1_WORDS:W1_WORDS + STAGE].rearrange("p (b m c) -> p b m c", b=2, m=M1)
        assert SHIFT * L1 <= STAGE
        xT_sb = sb("xT_sb", [PT, 2 * KT * C])
        xT = xT_sb[:, :].bitcast(f16).rearrange("p (b s k c) -> p b s k c", b=2, s=2, k=KT)
        nat = sb("nat", [PT, SLOTS, DP])
        squares_sb = sb("squares_sb", [PT, (D + 1) // 2])
        squares = squares_sb[:, :].bitcast(bf16)[:, 0:D]
        spread = sb("spread", [PT, 3, C])
        w2 = sb("w2", [PT, 2, M1, L2], f16)
        raw_f, wrap_f = (nat[:, SLOTS - 1, j * TILES * NT:(j + 1) * TILES * NT].rearrange(
            "p (t f) -> p t f", t=TILES) for j in range(2))
        raw = raw_f.bitcast(i32)
        ixf = nat[:, SLOTS - 1, 2 * TILES * NT:3 * TILES * NT].rearrange("p (t f) -> p t f", t=TILES)
        w2_raw = xT_sb[:, 0:M1 * L2].rearrange("p (k m) -> p k m", k=M1)
        w3 = squares_sb[:, 0:M2 * L3].bitcast(f16).rearrange("p (s k m) -> p s k m", s=2, k=M2)
        assert M1 * L2 <= KT * C
        w2e = squares_sb[:, 0:L2]
        w2e_k = [squares_sb[:, L2:2 * L2], nat[:, 2, DP - L2:DP]]
        BLOCK = M1 * NB
        h1r = [arena[:, j * BLOCK:(j + 1) * BLOCK].rearrange("p (b m c) -> p b m c", b=CB, m=M1)
               for j in range(2)]
        n1 = [place.bitcast(f16).rearrange("p (s k r) -> p s k r", s=2, k=M1) for place in (
            nat[:, 1:3, :].rearrange("p s f -> p (s f)")[:, 0:BLOCK],
            *(arena[:, (2 + j) * BLOCK:(3 + j) * BLOCK] for j in range(2)))]
        assert BLOCK + L2 <= 2 * DP
        AT3 = 4 * BLOCK
        w3_raw, w3_g = (arena[:, AT3 + j * M2 * L3:AT3 + (j + 1) * M2 * L3].rearrange(
            "p (k m) -> p k m", k=M2) for j in range(2))
        assert AT3 + 2 * M2 * L3 <= W1_WORDS
        h2T = xT_sb[:, 0:M2 * B].rearrange("p (m r) -> p m r", m=M2)
        n2 = arena[:, 0:M2 * B].bitcast(f16).rearrange("p (s k r) -> p s k r", s=2, k=M2)
        assert M2 * B <= 2 * BLOCK
        h3T = arena[:, W1_WORDS:W1_WORDS + M3 * B].rearrange("p (m r) -> p m r", m=M3)
        h3_part = arena[:, 2 * BLOCK:2 * BLOCK + 3 * M3 * B // 2].bitcast(bf16).rearrange(
            "p (s m r) -> p s m r", s=3, m=M3)
        h3_rest = arena[:, 2 * BLOCK + 3 * M3 * B // 2:2 * BLOCK + 3 * M3 * B // 2 + M3 * NB].rearrange(
            "p (m r) -> p m r", m=M3)
        assert 3 * M3 * B // 2 + M3 * NB <= 2 * BLOCK
        a_row = nat[:, SLOTS - 1, :]

        vec_sb = sb("vec_sb", [PT, vec.shape[1]])
        const_sb = sb("const_sb", [PT, const.shape[1]])
        ident = const_sb[:, 0:PT]
        table_base = const_sb[:, PT:PT + NT]
        ones = sb("ones", [PT, PT])
        index = sb("index", [PT, TILES, NT], i32)
        index_slot = sb("index_slot", [PT, SLOTS, NT], i32)
        part1 = sb("part1", [PT, 4])
        cc = sb("cc", [PT, 3])
        al = sb("al", [PT, KT, 2, 3], f16)
        mx_w1 = sb("mx_w1", [PT, 8])
        mx = sb("mx", [PT, 4])
        bound = sb("bound", [PT, 1])
        power = sb("power", [PT, 1], i32)
        rpower = sb("rpower", [PT, 1])
        sc_al, iv_al = sb("sc_al", [PT, 1]), sb("iv_al", [PT, 1])
        sc_w1, iv_w1 = sb("sc_w1", [PT, 1]), sb("iv_w1", [PT, 1])
        sc_w2, iv_w2 = sb("sc_w2", [PT, 1]), sb("iv_w2", [PT, 1])
        sc_w3, iv_w3 = sb("sc_w3", [PT, 1]), sb("iv_w3", [PT, 1])
        sc_x = sb("sc_x", [PT, 2, 2])
        iv_x = sb("iv_x", [PT, 2, 2])
        iv_h = sb("iv_h", [PT, 2, 2])
        iv_d = sb("iv_d", [PT, 2, 2])
        dot6 = sb("dot6", [PT, 2, 6])
        dot3 = sb("dot3", [PT, 2, 3])
        pqt = sb("pqt", [PT, 3, 2])
        p_in = sb("p_in", [PT, 2])
        cc_tmp = squares_sb[:, 0:3 * KT].rearrange("p (i k) -> p i k", i=3)
        rows = sb("rows", [PT, 3, TILES])
        ra, rf, rt, rq, r1, r2, r3 = (sb(f"r_{n}", [PT, 2]) for n in "aftq123")
        y_stats = sb("y_stats", [PT, KT, CHUNKS * BN])
        h1_stats = sb("h1_stats", [PT, M1, CHUNKS * BN])
        h2_stats = sb("h2_stats", [PT, M2, N2 * BN])
        h3_stats = sb("h3_stats", [PT, M3, N2 * BN])
        mvy = sb("mvy", [PT, KT, 2])
        mv1 = sb("mv1", [PT, M1, 2])
        mv2 = sb("mv2", [PT, M2, 2])
        mv3 = sb("mv3", [PT, M3, 2])
        bn_tmp = sb("bn_tmp", [PT, 5, KT])
        ay = sb("ay", [PT, KT])
        rs1, nb1 = sb("rs1", [PT, M1]), sb("nb1", [PT, M1])
        rs2, nb2 = sb("rs2", [PT, M2]), sb("nb2", [PT, M2])
        a3, a3_rest = sb("a3", [PT, M3]), sb("a3_rest", [PT, M3])
        a3_part = sb("a3_part", [PT, M3, 3], bf16)
        bias2 = sb("bias2", [PT, M2])
        bias3 = sb("bias3", [PT, M3])
        fin_tmp = sb("fin_tmp", [PT, 4, KT])
        fin_h = sb("fin_h", [PT, 3, M3])
        fin_sum = sb("fin_sum", [PT, 3])
        fin_part = sb("fin_part", [PT, 1])
        fin_c = sb("fin_c", [PT, 4])
        xa = sb("xa", [PT, TILES])
        z1, z2, z3, z4, z_h = (sb(f"z{n}", [PT, TILES]) for n in "1234h")
        zT = sb("zT", [TILES, PT])
        warm = sb("warm", [PT, 1])

        at = [0]

        def take(n):
            at[0] += n
            return vec_sb[:, at[0] - n:at[0]]

        alpha = take(3 * KT).rearrange("p (k i) -> p k i", i=3)
        b0, b1x, b2x = take(KT), take(KT), take(KT)
        gy, by, wy = take(KT), take(KT), take(KT)
        b1, g1, e1 = take(M1), take(M1), take(M1)
        b2, g2, e2 = take(M2), take(M2), take(M2)
        b3, g3, e3, w_h = take(M3), take(M3), take(M3), take(M3)
        bf = take(1)

        tp = [pb(f"tp{i}", [PT, NB]) for i in range(2)]
        acc = [pb(f"acc{i}", [PT, NB]) for i in range(2)]
        yb = [pb(f"yb{i}", [PT, NB]) for i in range(2)]
        turned = pb("turned", [PT, NB])
        tiny = pb("tiny", [PT, NB])
        banks = [*tp, *acc, *yb]
        spread_banks = [*yb, turned]
        SUM_W, SUM_X, DOT, FIN, HD = 4, 8, 16, 44, 64

        s_vec = sem("s_vec")
        s_raw = sem("s_raw")
        s_w1 = [sem(f"s_w1_{j}") for j in range(-(-KT // SHIFT))]
        s_w2 = sem("s_w2")
        s_w3 = sem("s_w3")
        s_ones = sem("s_ones")
        s_dve = sem("s_dve")
        s_row = sem("s_row")
        s_set = sem("s_set")
        s_index = sem("s_index")
        s_slot = sem("s_slot")
        s_started = sem("s_started")
        s_moving = sem("s_moving")
        s_pad = sem("s_pad")
        s_gath = [sem(f"s_gath{s}") for s in range(SLOTS)]
        s_num = [sem(f"s_num{s}") for s in range(SLOTS)]
        s_spill = [sem(f"s_spill{s}") for s in range(SLOTS)]
        s_wask = sem("s_wask")
        s_wsum = sem("s_wsum")
        s_ask = sem("s_ask")
        s_sum = sem("s_sum")
        s_w2p = sem("s_w2p")
        s_w2e = sem("s_w2e")
        s_shift2 = sem("s_shift2")
        s_w2g = sem("s_w2g")
        s_w2s = sem("s_w2s")
        s_w2f = sem("s_w2f")
        s_w2h = sem("s_w2h")
        s_w2l = sem("s_w2l")
        s_w1s = sem("s_w1s")
        s_w1h = sem("s_w1h")
        s_w1l = sem("s_w1l")
        s_scale = sem("s_scale")
        s_tp = sem("s_tp")
        s_hi = sem("s_hi")
        s_lo = sem("s_lo")
        s_dots = sem("s_dots")
        s_rownum = sem("s_rownum")
        s_bcast = sem("s_bcast")
        s_spread = sem("s_spread")
        s_ystep = sem("s_ystep")
        s_yused = sem("s_yused")
        s_acc = sem("s_acc")
        s_h1 = sem("s_h1")
        s_bn1 = sem("s_bn1")
        s_h1out = [sem(f"s_h1out{p}") for p in range(2)]
        s_var = sem("s_var")
        s_root = sem("s_root")
        s_ay = sem("s_ay")
        s_afull = sem("s_afull")
        s_arow = sem("s_arow")
        s_h1in = [sem(f"s_h1in{j}") for j in range(N2)]
        s_n1 = sem("s_n1")
        s_n1h = sem("s_n1h")
        s_n1l = sem("s_n1l")
        s_acc2 = sem("s_acc2")
        s_h2 = sem("s_h2")
        s_w3g = sem("s_w3g")
        s_w3s = sem("s_w3s")
        s_w3f = sem("s_w3f")
        s_w3h = sem("s_w3h")
        s_w3l = sem("s_w3l")
        s_shift3 = sem("s_shift3")
        s_bias3 = sem("s_bias3")
        s_n2 = sem("s_n2")
        s_n2h = sem("s_n2h")
        s_n2l = sem("s_n2l")
        s_acc3 = sem("s_acc3")
        s_h3 = sem("s_h3")
        s_h3a = sem("s_h3a")
        s_h3r = sem("s_h3r")
        s_h3b = sem("s_h3b")
        s_h3c = sem("s_h3c")
        s_h3_last = sem("s_h3_last")
        s_xin = [sem(f"s_xin{s}") for s in range(XSLOTS)]
        s_xa = sem("s_xa")
        s_fin1 = sem("s_fin1")
        s_fin1_ps = sem("s_fin1_ps")
        s_fin_in = sem("s_fin_in")
        s_a3 = sem("s_a3")
        s_fin_ps = sem("s_fin_ps")
        s_hd = sem("s_hd")
        s_z = sem("s_z")
        s_zT = sem("s_zT")
        s_zo = sem("s_zo")
        s_out = sem("s_out")

        block = ctx.enter_context(nc.Block())

        W1_FIRST, W1_SQUARES, W1_SECOND = 5, 15, 17
        DVE_BLOCKS = N2 - 2
        W2_AHEAD = 5
        EARLY1 = M1 - 2
        EARLY2 = M2 - 1
        DOTS_AT = 3
        SPREAD_AT = 25
        TILE0 = {66: (0, 0), 69: (0, 1), 82: (0, 2), 86: (0, 3), 90: (0, 4)}
        FIRST = ({70: 0, 140: 1}, {3: 0, 7: 1},
                 {**TILE0, 134: (1, 0), 137: (1, 1), 147: (1, 2), 149: (1, 3), 151: (1, 4)})
        OTHERS = ({70: 0, 130: 1}, {3: 0, 6: 1},
                  {**TILE0, 126: (1, 0), 129: (1, 1), 145: (1, 2), 148: (1, 3), 151: (1, 4)})
        assert len(TILE0) == GROUPS
        SHIFT2_AT, SUM_W2_AT = 76, 105
        L3_STEPS = [*((j, k) for k in range(M2) for j in range(2)), *((j, k) for j in range(2, N2) for k in range(M2))]

        def turns_between(turn_at, first, last):
            return [turn_at[t] for t in range(first, last) if t in turn_at]

        def width(g):
            return min(GK, KT - GK * g)

        def h1_block(j, k):
            return h1s[:, :, k, :] if j == 0 else h1r[(j - 1) % 2][:, :, k, :]

        start_banks = [*tp, *yb, turned]

        def tp_bank(c, j, g):
            return start_banks[g] if isinstance(c, int) and c == 0 else tp[(j + g) % 2]

        def n1_block(j):
            return n1[0] if j == 0 else n1[1 + (j - 1) % 2]

        @block.sync
        def _(sp):
            sp.dma_start(raw[:, :, :], cat).then_inc(s_raw, 16)
            sp.dma_start(vec_sb[:, :], vec).then_inc(s_vec, 16)
            sp.dma_start(const_sb[:, :], const).then_inc(s_vec, 16)
            for j in range(-(-KT // SHIFT)):
                k = slice(j * SHIFT, min(KT, (j + 1) * SHIFT))
                sp.dma_start(w1_raw[:, k, :], w1t[:, k, :]).then_inc(s_w1[j], 16)
            for s in range(SLOTS):
                sp.sem_inc(s_spill[s], 16)
            for p in range(2):
                sp.sem_inc(s_h1out[p], 16)

            def numerical(i, s):
                sp.wait_ge(s_hi, GROUPS * (SLOTS * i + s + 1))
                sp.sem_inc(s_moving, 1)
                sp.dma_start(nat[:, s, NT * E:D], num[ds((i * SLOTS + s) * PT, PT), :]).then_inc(s_num[s], 16)

            def spill(i, s):
                sp.wait_ge(s_gath[s], 16 * NT * (i + 1))
                sp.sem_inc(s_moving, 1)
                sp.dma_start(x_spill[ds((i * SLOTS + s) * PT, PT), :], nat[:, s, 0:NT * E]).then_inc(s_spill[s], 16)

            def h1_out(c, p):
                sp.wait_ge(s_h1, 2 + M1 * (c + 1))
                sp.sem_inc(s_moving, 1)
                sp.dma_start(h1_spill[ds(c, 1), :, :].rearrange("o p n -> (o p) n"),
                             h1s[:, p, :, :].rearrange("p m c -> p (m c)")).then_inc(s_h1out[p], 16)

            sp.wait_ge(s_pad, 2)
            for s in range(SLOTS):
                numerical(0, s)
            for s in range(SLOTS):
                spill(0, s)
            numerical(1, 0)
            numerical(1, 1)
            spill(1, 0)
            spill(1, 1)
            h1_out(0, 0)
            with sp.Fori(0, PAIRS - 2) as i:
                numerical(i + 1, 2)
                numerical(i + 1, 3)
                spill(i + 1, 2)
                spill(i + 1, 3)
                h1_out(2 * i + 1, 1)
                numerical(i + 2, 0)
                numerical(i + 2, 1)
                spill(i + 2, 0)
                spill(i + 2, 1)
                h1_out(2 * i + 2, 0)
            numerical(PAIRS - 1, 2)
            numerical(PAIRS - 1, 3)
            spill(PAIRS - 1, 2)
            spill(PAIRS - 1, 3)
            h1_out(CHUNKS - 3, 1)
            sp.wait_ge(s_acc, M1 * (1 + CHUNKS))
            sp.wait_ge(s_yused, 1 + CHUNKS)
            sp.dma_start(w2_raw[:, :, :], w2t).then_inc(s_w2, 16)
            for q in range(SLOTS):
                sp.wait_ge(s_spill[q], 16 + 16 * TILES // SLOTS)
            sp.wait_ge(s_hi, GROUPS * (SLOTS + TILES))

            def x_in(t):
                s = t % XSLOTS
                if t >= XSLOTS:
                    sp.wait_ge(s_xa, t - XSLOTS + 1)
                rows_t = slice(t * PT, (t + 1) * PT)
                sp.dma_start(nat[:, s, 0:NT * E], x_spill[rows_t, :]).then_inc(s_xin[s], 16)
                sp.dma_start(nat[:, s, NT * E:D], num[rows_t, :]).then_inc(s_xin[s], 16)

            def h1_in(j):
                for b in range(CB):
                    sp.dma_start(h1r[(j - 1) % 2][:, b, :, :].rearrange("p m c -> p (m c)"),
                                 h1_spill[ORDER[j] * CB + b, :, :]).then_inc(s_h1in[j], 16)

            x_in(0)
            sp.wait_ge(s_acc, M1 * (2 + CHUNKS))
            for p in range(2):
                sp.wait_ge(s_h1out[p], 16 + 16 * (PAIRS - 1))
            h1_in(1)
            h1_in(2)
            sp.dma_start(w3_raw[:, :, :], w3t).then_inc(s_w3, 16)
            sp.wait_ge(s_acc2, M2)
            for t in range(1, XSLOTS):
                x_in(t)
            sp.wait_ge(s_n1l, M1 * 2)
            h1_in(3)
            for t in range(XSLOTS, TILES):
                x_in(t)
            sp.wait_ge(s_zo, 1)
            sp.dma_start(out.rearrange("(t p) o -> t (p o)", p=PT), zT[:, :]).then_inc(s_out, 16)
            sp.wait_ge(s_out, 16)

        @block.gpsimd
        def _(pool):
            nc.gpsimd.memset(nat[:, 0:SLOTS - 1, NT * E:DP], 0.0).then_inc(s_pad, 1)
            nc.gpsimd.memset(nat[:, SLOTS - 1, NT * E:DP], 0.0).then_inc(s_pad, 1)
            pool.wait_ge(s_index, 1)
            with pool.Fori(0, TILES // SLOTS) as i:
                for s in range(SLOTS):
                    if s == 1:
                        pool.wait_ge(s_index, 2)
                    pool.wait_ge(s_hi, GROUPS * (SLOTS * i + s + 1))
                    pool.wait_ge(s_spill[s], 16 * i + 16)
                    nc.gpsimd.tensor_copy(index_slot[:, s, :],
                                          index[:, ds(i * SLOTS + s, 1), :].rearrange("p a f -> p (a f)")
                                          ).then_inc(s_slot, 1)
                    pool.wait_ge(s_slot, SLOTS * i + s + 1)
                    pool.sem_inc(s_started, 1)
                    for f in range(NT):
                        nc.gpsimd.indirect_dma_start(
                            nat[:, s, f * E:(f + 1) * E], None, table_rows,
                            bass.IndirectOffsetOnAxis(ap=index_slot[:, s, f:f + 1], axis=0),
                        ).then_inc(s_gath[s], 16)

            for k in range(1, M1):
                pool.wait_ge(s_w2p, k + 1)
                if k > 1:
                    pool.wait_ge(s_w2e, k - 1)
                nc.gpsimd.tensor_tensor(w2e, w2e, w2e_k[k % 2], ALU.add).then_inc(s_w2e, 1)

            def lower_w2(some):
                for k in some:
                    nc.gpsimd.tensor_tensor(w2[:, 1, k, :], w2_raw[:, k, :], w2[:, 0, k, :],
                                            ALU.subtract).then_inc(s_w2l, 1)

            pool.wait_ge(s_w2h, 1)
            lower_w2(range(W2_AHEAD))

            def lower1(j):
                if j == 3:
                    pool.wait_ge(s_acc2, M2 * 2)
                for k in range(M1):
                    if j == 0 and W2_AHEAD - 1 + k in range(W2_AHEAD, M1):
                        lower_w2([W2_AHEAD - 1 + k])
                    pool.wait_ge(s_n1h, M1 * j + k + 1)
                    nc.gpsimd.tensor_tensor(n1_block(j)[:, 1, k, :].rearrange("p (b c) -> p b c", b=CB), h1_block(j, k),
                                            n1_block(j)[:, 0, k, :].rearrange("p (b c) -> p b c", b=CB),
                                            ALU.subtract).then_inc(s_n1l, 1)

            lower1(0)
            for j in range(1, N2):
                lower1(j)
            pool.wait_ge(s_w3h, 1)
            nc.gpsimd.tensor_tensor(w3[:, 1, :, :], w3_g[:, :, :], w3[:, 0, :, :], ALU.subtract).then_inc(s_w3l, 1)
            for n, (j, k) in enumerate(L3_STEPS):
                r = slice(ORDER[j] * NB, (ORDER[j] + 1) * NB)
                pool.wait_ge(s_n2h, n + 1)
                nc.gpsimd.tensor_tensor(n2[:, 1, k, r], h2T[:, k, r], n2[:, 0, k, r], ALU.subtract).then_inc(s_n2l, 1)
            pool.wait_ge(s_h3c, M3 * DVE_BLOCKS)
            for j in range(DVE_BLOCKS, N2):
                r = slice(ORDER[j] * NB, (ORDER[j] + 1) * NB)
                for m in range(M3):
                    if j > DVE_BLOCKS:
                        pool.wait_ge(s_h3_last, M3 * (j - 1 - DVE_BLOCKS) + m + 1)
                    pool.wait_ge(s_h3a, len(banks) + M3 * j + m + 1)
                    nc.gpsimd.tensor_tensor(h3_rest[:, m, :], h3T[:, m, r], h3_part[:, 0, m, r],
                                            ALU.subtract).then_inc(s_h3r, 1)
                for m in range(M3):
                    pool.wait_ge(s_h3b, M3 * j + m + 1)
                    nc.gpsimd.tensor_tensor(h3_part[:, 2, m, r], h3_rest[:, m, :], h3_part[:, 1, m, r],
                                            ALU.subtract).then_inc(s_h3_last, 1)

        @block.scalar
        def _(act):
            act.sem_inc(s_h1, 2)

            def upper(c, p, j, g):
                if g == 0:
                    act.wait_ge(s_scale, 2 * c + j + 1)
                    if j == 0:
                        act.wait_ge(s_acc, M1 * (c + 1))
                        act.wait_ge(s_yused, c + 1)
                act.wait_ge(s_tp, GROUPS * (SLOTS + 2 * c + j) + g + 1)
                n = width(g)
                nc.scalar.activation(xT[:, p, 0, GK * g:GK * g + n, j * PT:(j + 1) * PT],
                                     tp_bank(c, j, g)[:, 0:n * PT].rearrange("p (k r) -> p k r", k=n),
                                     ACT.Copy, scale=sc_x[:, p, j:j + 1]).then_inc(s_hi, 1)

            def relu_h1(c, p, m):
                act.wait_ge(s_acc, M1 * (c + 2) + m + 1)
                if m == 0:
                    act.wait_ge(s_h1out[p], (c - p) * 8 + 16)
                    act.wait_ge(s_bn1, c + 1)
                for j in range(2):
                    r = slice(j * PT, (j + 1) * PT)
                    last = nc.scalar.activation(h1s[:, p, m, r], acc[m % 2][:, r], ACT.Relu,
                                                bias=b1[:, m:m + 1], scale=iv_h[:, p, j:j + 1])
                last.then_inc(s_h1, 1)

            def sum_squares(s, j, i):
                act.wait_ge(s_gath[s], 16 * NT * (i + 1))
                act.wait_ge(s_num[s], 16 * (i + 1))
                twin = (KT - 1) * PT + TWIN
                nc.scalar.copy(nat[:, s, twin:twin + LAST], nat[:, s, D - LAST:D])
                nc.scalar.activation(squares[:, :], nat[:, s, 0:D], ACT.Square,
                                     accum_out=mx[:, j:j + 1]).then_inc(s_ask, 1)

            def spread_rows(c):
                act.wait_ge(s_bcast, c + 1)
                nc.scalar.copy(spread[:, 0:2, :], yb[0][:, :].rearrange("p (i r) -> p i r", i=2))
                nc.scalar.copy(spread[:, 2, :], yb[1][:, 0:C]).then_inc(s_spread, 1)

            def chunk(c, p, i_next, schedule):
                sum_at, squares_ahead_of, turn_at = schedule
                spread_rows(c)
                for m in range(M1):
                    if m in squares_ahead_of:
                        j = squares_ahead_of[m]
                        sum_squares(2 * (1 - p) + j, j, i_next)
                    for j, g in turns_between(turn_at, KT * m, KT * (m + 1)):
                        upper(c + 1, 1 - p, j, g)
                    relu_h1(c, p, m)

            def root(n, k):
                act.wait_ge(s_var, n)
                nc.scalar.activation(bn_tmp[:, 1, 0:k], bn_tmp[:, 0, 0:k], ACT.Sqrt).then_inc(s_root, 1)

            act.sem_inc(s_hi, GROUPS * SLOTS)
            act.sem_inc(s_h2, M2)
            act.wait_ge(s_ones, 1)
            nc.scalar.activation(warm[:, :], ones[:, 0:1], ACT.Square)
            act.wait_ge(s_vec, 32)
            act.wait_ge(s_w1s, 1)

            def upper_w1(k):
                if k >= SHIFT:
                    act.wait_ge(s_w1l, k - SHIFT + 1)
                nc.scalar.activation(w1[:, k, 0, :], w1_raw[:, k, :], ACT.Copy,
                                     scale=sc_w1[:, 0:1]).then_inc(s_w1h, 1)

            for k in range(2):
                upper_w1(k)
            act.wait_ge(s_wsum, 1)
            sum_squares(0, 0, 0)
            for k in range(2, W1_FIRST):
                upper_w1(k)
            for g in range(GROUPS):
                upper(0, 0, 0, g)
            for k in range(W1_FIRST, W1_SQUARES):
                upper_w1(k)
            sum_squares(1, 1, 0)
            for k in range(W1_SQUARES, W1_SECOND):
                upper_w1(k)
            for g in range(GROUPS):
                upper(0, 0, 1, g)
            for k in range(W1_SECOND, KT):
                upper_w1(k)
            def upper1(j, some=range(M1)):
                if j == 3 and some[0] == 0:
                    act.wait_ge(s_acc2, M2 * 2)
                for k in some:
                    act.wait_ge(s_n1, M1 * j + k + 1)
                    nc.scalar.copy(n1_block(j)[:, 0, k, :].rearrange("p (b c) -> p b c", b=CB),
                                   h1_block(j, k)).then_inc(s_n1h, 1)

            chunk(0, 0, 0, FIRST)
            with act.Fori(0, PAIRS - 1) as i:
                chunk(2 * i + 1, 1, i + 1, OTHERS)
                chunk(2 * i + 2, 0, i + 1, OTHERS)
            spread_rows(CHUNKS - 1)
            for m in range(M1):
                relu_h1(CHUNKS - 1, 1, m)
                if m == 1:
                    act.wait_ge(s_w2, 16)
                    for k in range(M1):
                        if k > 2:
                            act.wait_ge(s_w2e, k - 2)
                        nc.scalar.activation(w2e if k == 0 else w2e_k[k % 2], w2_raw[:, k, :], ACT.Copy,
                                             scale=e1[:, k:k + 1]).then_inc(s_w2p, 1)
                if m == 2:
                    act.wait_ge(s_w2p, M1)
                    for k in range(M1):
                        nc.scalar.activation(w2_raw[:, k, :], w2_raw[:, k, :], ACT.Copy,
                                             scale=g1[:, k:k + 1]).then_inc(s_w2g, 1)
                if m == 4:
                    act.wait_ge(s_w2s, 1)
                    nc.scalar.activation(w2_raw[:, :, :], w2_raw[:, :, :], ACT.Copy, scale=sc_w2[:, 0:1]).then_inc(s_w2f, 1)
                    act.wait_ge(s_w2f, 1)
                    nc.scalar.copy(w2[:, 0, :, :], w2_raw[:, :, :]).then_inc(s_w2h, 1)
                if m == 5:
                    nc.scalar.activation(warm[:, :], ones[:, 0:1], ACT.Sqrt)
                if m == 6:
                    root(1, EARLY1)
                    upper1(0, range(EARLY1 - 1))

            def relu_h2(j, some=range(M2)):
                for m in some:
                    act.wait_ge(s_acc2, M2 * j + m + 1)
                    nc.scalar.activation(h2T[:, m, ORDER[j] * NB:(ORDER[j] + 1) * NB], banks[m][:, :], ACT.Relu,
                                         bias=bias2[:, m:m + 1], scale=iv_w2[:, 0:1]).then_inc(s_h2, 1)

            upper1(0, range(EARLY1 - 1, EARLY1))
            root(2, M1 - EARLY1)
            upper1(0, range(EARLY1, M1))
            upper1(1)
            root(3, KT)
            relu_h2(0)
            for g in range(GROUPS):
                act.wait_ge(s_afull, g + 1)
                nc.scalar.copy(a_row[:, GK * g * PT:(GK * g + width(g)) * PT],
                               spread_banks[g % 3][:, 0:width(g) * PT]).then_inc(s_arow, 1)
            act.wait_ge(s_w3, 16)
            for k in range(M2):
                nc.scalar.activation(w3_g[:, k, :], w3_raw[:, k, :], ACT.Copy,
                                     scale=g2[:, k:k + 1]).then_inc(s_w3g, 1)
            upper1(2)
            relu_h2(1)
            upper1(3)
            act.wait_ge(s_w3s, 1)
            nc.scalar.activation(w3_g[:, :, :], w3_g[:, :, :], ACT.Copy, scale=sc_w3[:, 0:1]).then_inc(s_w3f, 1)
            act.wait_ge(s_w3f, 1)
            nc.scalar.copy(w3[:, 0, :, :], w3_g[:, :, :]).then_inc(s_w3h, 1)
            relu_h2(2)
            relu_h2(3, range(EARLY2))
            root(4, EARLY2)

            def upper2(n):
                j, k = L3_STEPS[n]
                r = slice(ORDER[j] * NB, (ORDER[j] + 1) * NB)
                act.wait_ge(s_n2, n + 1)
                nc.scalar.copy(n2[:, 0, k, r], h2T[:, k, r]).then_inc(s_n2h, 1)

            def out_h3(j):
                r = slice(ORDER[j] * NB, (ORDER[j] + 1) * NB)
                for place, s_done in ((h3T, s_h3), (h3_part[:, 0, :, :], s_h3a)):
                    for m in range(M3):
                        act.wait_ge(s_acc3, M3 * j + m + 1)
                        nc.scalar.activation(place[:, m, r], banks[(M3 * j + m) % len(banks)][:, :], ACT.Identity,
                                             bias=bias3[:, m:m + 1], scale=iv_w3[:, 0:1]).then_inc(s_done, 1)

            def second_part(j):
                for m in range(M3):
                    act.wait_ge(s_h3r, M3 * j + m + 1)
                    nc.scalar.copy(h3_part[:, 1, m, ORDER[j] * NB:(ORDER[j] + 1) * NB],
                                   h3_rest[:, m, :]).then_inc(s_h3b, 1)

            act.sem_inc(s_h3a, len(banks))
            for n in range(2 * EARLY2):
                upper2(n)
                if n == 1:
                    relu_h2(3, range(EARLY2, M2))
            root(5, M2 - EARLY2)
            for n in range(2 * EARLY2, len(L3_STEPS)):
                upper2(n)
            act.wait_ge(s_bias3, 1)
            for j in range(N2 - 1):
                out_h3(j)
                second_part(j)
            out_h3(N2 - 1)
            root(6, M3)
            second_part(N2 - 1)
            nc.scalar.activation(warm[:, :], ones[:, 0:1], ACT.Sigmoid)
            act.wait_ge(s_zT, 1)
            nc.scalar.activation(zT[:, :], turned[0:TILES, 0:PT], ACT.Sigmoid).then_inc(s_zo, 1)

        @block.vector
        def _(dve):
            v = nc.vector
            done = [0]

            def link(ins):
                done[0] += 1
                ins.then_inc(s_dve, 1)
                dve.wait_ge(s_dve, done[0])

            def largest(out, in_, axis=AX.X):
                return v.tensor_reduce(out, in_, axis, ALU.max, apply_absolute_value=True)

            def scale_of(linked, col, squared=False):
                linked(v.tensor_scalar(bound[:, :], col, TINY, None, ALU.max))
                bits = bound[:, :].bitcast(i32)
                if squared:
                    linked(v.tensor_scalar(power[:, :], bits, EXPONENT, 1, ALU.bitwise_and, ALU.logical_shift_right))
                    linked(v.tensor_scalar(power[:, :], power[:, :], float(BIAS), None, ALU.add))
                    bits = power[:, :]
                linked(v.tensor_scalar(power[:, :], bits, EXPONENT, None, ALU.bitwise_and))
                linked(v.reciprocal(rpower[:, :], power[:, :].bitcast(f32)))

            def weight_scale(col, sc, iv, factor):
                scale_of(link, col)
                link(v.tensor_scalar(sc[:, :], rpower[:, :], 2.0 ** ROOM, None, ALU.mult))
                link(v.tensor_scalar(iv[:, :], power[:, :].bitcast(f32), factor * 2.0 ** -ROOM, None, ALU.mult))

            dve.sem_inc(s_bn1, 2)
            dve.sem_inc(s_lo, 2)
            dve.sem_inc(s_yused, 2)
            dve.wait_ge(s_raw, 16)
            dve.wait_ge(s_vec, 32)
            for t in (slice(0, 1), slice(1, TILES)):
                n = t.stop - t.start
                link(v.tensor_copy(ixf[:, t, :], raw[:, t, :]))
                link(v.tensor_scalar(wrap_f[:, t, :], ixf[:, t, :], 0.0, float(V), ALU.is_lt, ALU.mult))
                link(v.tensor_tensor(ixf[:, t, :], ixf[:, t, :], wrap_f[:, t, :], ALU.add))
                link(v.tensor_scalar(ixf[:, t, :], ixf[:, t, :], 0.0, float(V - 1), ALU.max, ALU.min))
                v.tensor_tensor(index[:, t, :], ixf[:, t, :],
                                table_base.unsqueeze(1).broadcast_to([PT, n, NT]), ALU.add).then_inc(s_index, 1)
            v.memset(ones[:, :], 1.0).then_inc(s_ones, 1)
            link(v.tensor_tensor(cc_tmp[:, 0, :], b0, alpha[:, :, 1], ALU.mult))
            link(v.tensor_tensor(cc_tmp[:, 1, :], b0, alpha[:, :, 2], ALU.mult))
            link(v.tensor_tensor(cc_tmp[:, 2, :], b1x, alpha[:, :, 2], ALU.mult))
            v.reduce_sum(part1[:, 0:3], cc_tmp[:, :, :], axis=AX.X)
            largest(part1[:, 3:4], vec_sb[:, 0:3 * KT]).then_inc(s_wask, 1)
            dve.wait_ge(s_wsum, 1)
            link(v.tensor_copy(cc[:, :], tiny[:, 0:3]))
            weight_scale(tiny[:, 3:4], sc_al, iv_al, 1.0)
            link(v.tensor_scalar(al[:, :, 0, :], alpha, sc_al[:, 0:1], None, ALU.mult))
            link(v.scalar_tensor_tensor(out=al[:, :, 1, :], in0=alpha, scalar=sc_al[:, 0:1], in1=al[:, :, 0, :],
                                        op0=ALU.mult, op1=ALU.subtract))
            for j in range(len(s_w1)):
                dve.wait_ge(s_w1[j], 16)
                k = slice(j * SHIFT, min(KT, (j + 1) * SHIFT))
                last = largest(mx_w1[:, j:j + 1], w1_raw[:, k, :].rearrange("p k m -> p (k m)"))
            link(last)
            v.reduce_max(mx[:, 2:3], mx_w1[:, 0:len(s_w1)], axis=AX.X).then_inc(s_wask, 1)
            dve.wait_ge(s_wsum, 2)
            weight_scale(tiny[:, SUM_W:SUM_W + 1], sc_w1, iv_w1, 1.0)
            dve.sem_inc(s_w1s, 1)

            SET_LINKS = 6

            def tile_scale(c, p, j):
                t = 2 * c + j
                local = [0]

                def set_link(ins):
                    local[0] += 1
                    ins.then_inc(s_set, 1)
                    dve.wait_ge(s_set, SET_LINKS * t + local[0])

                dve.wait_ge(s_sum, t + 1)
                scale_of(set_link, tiny[:, SUM_X + j:SUM_X + j + 1], squared=True)
                v.tensor_scalar(sc_x[:, p, j:j + 1], rpower[:, :], 2.0 ** ROOM, None, ALU.mult)
                v.tensor_scalar(iv_x[:, p, j:j + 1], power[:, :].bitcast(f32), 2.0 ** -ROOM, None, ALU.mult)
                v.tensor_scalar(iv_h[:, p, j:j + 1], power[:, :].bitcast(f32), 2.0 ** -ROOM, iv_w1[:, 0:1],
                                ALU.mult, ALU.mult)
                set_link(v.tensor_scalar(iv_d[:, p, j:j + 1], power[:, :].bitcast(f32), 2.0 ** -ROOM, iv_al[:, 0:1],
                                         ALU.mult, ALU.mult))
                dve.sem_inc(s_scale, 1)

            def lower(c, p, j, g):
                dve.wait_ge(s_hi, GROUPS * (SLOTS + 2 * c + j) + g + 1)
                n = width(g)
                part = [xT[:, p, q, GK * g:GK * g + n, j * PT:(j + 1) * PT] for q in range(2)]
                v.scalar_tensor_tensor(out=part[1], in0=tp_bank(c, j, g)[:, 0:n * PT].rearrange("p (k r) -> p k r", k=n),
                                       scalar=sc_x[:, p, j:j + 1], in1=part[0],
                                       op0=ALU.mult, op1=ALU.subtract).then_inc(s_lo, 1)

            def lower_w1(k):
                dve.wait_ge(s_w1h, k + 1)
                q, part = (slice(TWIN, PT), 0) if k == KT - 1 else (slice(0, PT), 1)
                v.scalar_tensor_tensor(out=w1[q, k, part, :], in0=w1_raw[q, k, :], scalar=sc_w1[q, 0:1],
                                       in1=w1[q, k, 0, :], op0=ALU.mult, op1=ALU.subtract).then_inc(s_w1l, 1)

            for k in range(3):
                lower_w1(k)
            tile_scale(0, 0, 0)
            for k in range(3, W1_FIRST):
                lower_w1(k)
            for g in range(GROUPS):
                lower(0, 0, 0, g)
            for k in range(W1_FIRST, W1_SECOND - 1):
                lower_w1(k)
            tile_scale(0, 0, 1)
            for g in range(GROUPS):
                lower(0, 0, 1, g)
            for k in range(W1_SECOND - 1, KT):
                lower_w1(k)

            LINKS = 12
            Y_STEPS = 3 * YBLOCKS + 2 * KT

            def row_numbers(c, p):
                local = [0]

                def row_link(ins):
                    local[0] += 1
                    ins.then_inc(s_row, 1)
                    dve.wait_ge(s_row, LINKS * c + local[0])

                dve.wait_ge(s_dots, c + 1)
                row_link(v.tensor_copy(dot6[:, :, :], tiny[:, DOT:DOT + 16].rearrange("p (j i) -> p j i", i=8)[:, :, 0:6]))
                row_link(v.tensor_tensor(dot3[:, :, :], dot6[:, :, 0:3], dot6[:, :, 3:6], ALU.add))
                row_link(v.tensor_tensor(dot3[:, :, :], dot3[:, :, :],
                                         iv_d[:, p, :].unsqueeze(2).broadcast_to([PT, 2, 3]), ALU.mult))
                row_link(v.tensor_scalar(ra[:, :], dot3[:, :, 0], 1.0, None, ALU.add))
                v.tensor_tensor(r2[:, :], ra[:, :], dot3[:, :, 2], ALU.mult)
                row_link(v.tensor_tensor(r1[:, :], ra[:, :], dot3[:, :, 1], ALU.mult))
                row_link(v.tensor_scalar(rf[:, :], r1[:, :], cc[:, 0:1], 1.0, ALU.add, ALU.add))
                row_link(v.scalar_tensor_tensor(out=r3[:, :], in0=r2[:, :], scalar=cc[:, 1:2], in1=rf[:, :],
                                                op0=ALU.add, op1=ALU.mult))
                row_link(v.tensor_scalar(rt[:, :], r3[:, :], cc[:, 2:3], 1.0, ALU.add, ALU.add))
                v.tensor_scalar(pqt[:, 2, :], rt[:, :], -1.0, None, ALU.add)
                row_link(v.tensor_tensor(rq[:, :], rf[:, :], rt[:, :], ALU.mult))
                v.tensor_scalar(pqt[:, 1, :], rq[:, :], -1.0, None, ALU.add)
                row_link(v.tensor_tensor(pqt[:, 0, :], ra[:, :], rq[:, :], ALU.mult))
                row_link(v.tensor_tensor(p_in[:, :], pqt[:, 0, :], iv_x[:, p, :], ALU.mult))
                dve.sem_inc(s_rownum, 1)
                row_link(v.tensor_copy(rows[:, :, ds(2 * c, 2)], pqt[:, :, :]))
                assert local[0] == LINKS, local[0]

            def y_pair(c, p, h):
                before = Y_STEPS * c + sum(3 + 2 * min(YK, KT - YK * g) for g in range(2 * h))
                blocks = [(g, min(YK, KT - YK * g), yb[g % 2]) for g in (2 * h, 2 * h + 1)]
                local = [0]
                mark = [0, 0]

                def step(q, ins):
                    local[0] += 1
                    mark[q] = local[0]
                    ins.then_inc(s_ystep, 1)

                for q, (g, n, y) in enumerate(blocks):
                    if h:
                        dve.wait_ge(s_ystep, before + q - 1)
                    step(q, v.tensor_tensor(y[:, 0:n * C].rearrange("p (k r) -> p k r", k=n),
                                            xT[:, p, 0, YK * g:YK * g + n, :], xT[:, p, 1, YK * g:YK * g + n, :],
                                            ALU.add))
                for q, (g, n, y) in enumerate(blocks):
                    yk = y[:, 0:n * C].rearrange("p (k r) -> p k r", k=n)
                    dve.wait_ge(s_ystep, before + mark[q])
                    step(q, v.tensor_tensor(yk, yk, spread[:, 0, :].unsqueeze(1).broadcast_to([PT, n, C]), ALU.mult))
                for row, b in ((1, b0), (2, b1x)):
                    for q, (g, n, y) in enumerate(blocks):
                        dve.wait_ge(s_ystep, before + mark[q])
                        for k in range(n):
                            yk = y[:, k * C:(k + 1) * C]
                            step(q, v.scalar_tensor_tensor(out=yk, in0=spread[:, row, :],
                                                           scalar=b[:, YK * g + k:YK * g + k + 1], in1=yk,
                                                           op0=ALU.mult, op1=ALU.add))
                for q, (g, n, y) in enumerate(blocks):
                    dve.wait_ge(s_ystep, before + mark[q])
                    for k in range(n):
                        last = v.bn_stats(y_stats[:, YK * g + k, ds(c * BN, BN)], y[:, k * C:(k + 1) * C])
                    step(q, last)

            def h1_statistics(c, p, some):
                for m in some:
                    dve.wait_ge(s_h1, 2 + M1 * c + m + 1)
                    last = v.bn_stats(h1_stats[:, m, ds(c * BN, BN)], h1s[:, p, m, :])
                return last

            def y_done(c):
                dve.wait_ge(s_ystep, Y_STEPS * (c + 1))
                dve.sem_inc(s_yused, 1)

            def chunk(c, p, rest):
                if rest is not None:
                    rest(c - 1, 1 - p)
                row_numbers(c, p)
                if rest is not None:
                    rest_h1(c - 1, 1 - p)
                dve.wait_ge(s_spread, c + 1)
                for h in range(2):
                    y_pair(c, p, h)
                tile_scale(c + 1, 1 - p, 0)
                for g in range(GROUPS):
                    lower(c + 1, 1 - p, 0, g)
                for h in range(2, YBLOCKS // 2 - 1):
                    y_pair(c, p, h)
                tile_scale(c + 1, 1 - p, 1)
                h1_statistics(c, p, range(2))
                for g in range(GROUPS):
                    if g >= 2:
                        h1_statistics(c, p, [g])
                    lower(c + 1, 1 - p, 1, g)

            def rest_y(c, p):
                y_pair(c, p, YBLOCKS // 2 - 1)
                y_done(c)

            def rest_h1(c, p):
                h1_statistics(c, p, range(GROUPS, M1)).then_inc(s_bn1, 1)

            def inverse_root(n, var, k):
                t = [bn_tmp[:, j, 0:k] for j in range(5)]
                link(v.tensor_scalar(t[0], var, EPS, None, ALU.add))
                dve.sem_inc(s_var, 1)
                dve.wait_ge(s_root, n)
                link(v.reciprocal(t[2], t[1]))
                link(v.tensor_tensor(t[3], t[2], t[2], ALU.mult))
                link(v.tensor_tensor(t[3], t[3], t[0], ALU.mult))
                link(v.tensor_scalar(t[3], t[3], -0.5, 1.5, ALU.mult, ALU.add))
                link(v.tensor_tensor(t[4], t[2], t[3], ALU.mult))
                return t[4]

            def aggregate(mv, stats, k):
                for j in range(k):
                    last = v.bn_aggr(mv[:, j, :], stats[:, j, :])
                link(last)

            def fold_y():
                aggregate(mvy, y_stats, KT)
                r = inverse_root(3, mvy[:, :, 1], KT)
                link(v.tensor_tensor(ay[:, :], r, gy, ALU.mult))
                link(v.tensor_tensor(ay[:, :], ay[:, :], wy, ALU.mult))
                dve.sem_inc(s_ay, 1)

            def cross_constants():
                link(v.tensor_tensor(fin_tmp[:, 0, :], b0, ay[:, :], ALU.mult))
                link(v.tensor_tensor(fin_tmp[:, 1, :], b1x, ay[:, :], ALU.mult))
                link(v.tensor_tensor(fin_tmp[:, 3, :], mvy[:, :, 0], b2x, ALU.add))
                link(v.tensor_tensor(fin_tmp[:, 3, :], b2x, fin_tmp[:, 3, :], ALU.subtract))
                link(v.tensor_tensor(fin_tmp[:, 3, :], fin_tmp[:, 3, :], ay[:, :], ALU.mult))
                link(v.tensor_tensor(fin_tmp[:, 2, :], by, wy, ALU.mult))
                link(v.tensor_tensor(fin_tmp[:, 2, :], fin_tmp[:, 2, :], fin_tmp[:, 3, :], ALU.add))
                link(v.reduce_sum(fin_sum[:, 0:3], fin_tmp[:, 0:3, :], axis=AX.X))
                dve.sem_inc(s_fin1, 1)

            def bound_w2():
                dve.wait_ge(s_shift2, 1)
                link(v.tensor_tensor(bias2[:, :], turned[:, 0:M2], b2, ALU.add))
                dve.wait_ge(s_w2g, M1)
                largest(mx[:, 2:3], w2_raw[:, :, :].rearrange("p k m -> p (k m)")).then_inc(s_wask, 1)
                dve.wait_ge(s_wsum, 3)
                weight_scale(tiny[:, SUM_W:SUM_W + 1], sc_w2, iv_w2, 1.0 / NSCALE)
                dve.sem_inc(s_w2s, 1)

            def bound_w3():
                dve.wait_ge(s_shift3, 1)
                link(v.tensor_tensor(bias3[:, :], turned[:, 0:M3], b3, ALU.add))
                dve.sem_inc(s_bias3, 1)
                dve.wait_ge(s_w3g, M2)
                largest(mx[:, 3:4], w3_g[:, :, :].rearrange("p k m -> p (k m)")).then_inc(s_wask, 1)

            def scale_w3():
                dve.wait_ge(s_wsum, 4)
                weight_scale(tiny[:, SUM_W:SUM_W + 1], sc_w3, iv_w3, 1.0 / NSCALE)
                dve.sem_inc(s_w3s, 1)

            def fold(n, mv, stats, some, rs, nb):
                q = slice(some[0], some[-1] + 1)
                aggregate(mv[:, q, :], stats[:, q, :], len(some))
                r = inverse_root(n, mv[:, q, 1], len(some))
                link(v.tensor_scalar(rs[:, q], r, NSCALE, None, ALU.mult))
                link(v.scalar_tensor_tensor(out=nb[:, q], in0=mv[:, q, 0], scalar=-1.0, in1=rs[:, q],
                                            op0=ALU.mult, op1=ALU.mult))

            def normalise1(j, some=range(M1)):
                if j:
                    dve.wait_ge(s_h1in[j], 16 * CB)
                for k in some:
                    v.tensor_scalar(h1_block(j, k), h1_block(j, k), rs1[:, k:k + 1], nb1[:, k:k + 1],
                                    ALU.mult, ALU.add).then_inc(s_n1, 1)

            def read_out(t):
                s = t % XSLOTS
                dve.wait_ge(s_xin[s], 32 * (t // XSLOTS + 1))
                v.tensor_tensor_reduce(out=nat[:, s, 0:D], in0=nat[:, s, 0:D], in1=a_row[:, 0:D],
                                       scale=1.0, scalar=0.0, op0=ALU.mult, op1=ALU.add,
                                       accum_out=xa[:, t:t + 1]).then_inc(s_xa, 1)

            def h2_statistics(j, some):
                for m in some:
                    dve.wait_ge(s_h2, M2 * (j + 1) + m + 1)
                    last = v.bn_stats(h2_stats[:, m, j * BN:(j + 1) * BN],
                                      h2T[:, m, ORDER[j] * NB:(ORDER[j] + 1) * NB])
                return last

            def normalise2(steps):
                for j, k in steps:
                    r = slice(ORDER[j] * NB, (ORDER[j] + 1) * NB)
                    v.tensor_scalar(h2T[:, k, r], h2T[:, k, r], rs2[:, k:k + 1], nb2[:, k:k + 1],
                                    ALU.mult, ALU.add).then_inc(s_n2, 1)

            chunk(0, 0, None)
            with dve.Fori(0, PAIRS - 1) as i:
                chunk(2 * i + 1, 1, rest_y)
                chunk(2 * i + 2, 0, rest_y)
            c = CHUNKS - 1
            rest_y(c - 1, 0)
            row_numbers(c, 1)
            rest_h1(c - 1, 0)
            dve.wait_ge(s_spread, c + 1)
            for h in range(YBLOCKS // 2 - 1):
                y_pair(c, 1, h)
                if h == 2:
                    bound_w2()
            link(h1_statistics(c, 1, range(EARLY1)))
            fold(1, mv1, h1_stats, range(EARLY1), rs1, nb1)
            normalise1(0, range(EARLY1))
            link(h1_statistics(c, 1, range(EARLY1, M1)))
            fold(2, mv1, h1_stats, range(EARLY1, M1), rs1, nb1)
            normalise1(0, range(EARLY1, M1))
            rest_y(c, 1)
            normalise1(1)
            fold_y()
            cross_constants()
            normalise1(2)
            h2_statistics(0, range(M2))
            dve.wait_ge(s_arow, GROUPS)
            read_out(0)
            later = iter(range(1, TILES))
            for j in range(1, N2):
                if j == 2:
                    scale_w3()
                reads = (TILES - 2) // (N2 - 1) + (j < N2 - 1)
                for n in range(reads):
                    read_out(next(later))
                    if j == N2 - 1 and n in (0, reads - 1):
                        h2_statistics(j, [n // (reads - 1)])
                if j == 1:
                    normalise1(3)
                    bound_w3()
                if j < N2 - 1:
                    h2_statistics(j, range(M2))
            link(h2_statistics(N2 - 1, range(2, EARLY2)))
            fold(4, mv2, h2_stats, range(EARLY2), rs2, nb2)
            normalise2(L3_STEPS[0:2 * EARLY2])
            link(h2_statistics(N2 - 1, range(EARLY2, M2)))
            fold(5, mv2, h2_stats, range(EARLY2, M2), rs2, nb2)
            normalise2(L3_STEPS[2 * EARLY2:])
            def z_without_h3():
                for t in later:
                    read_out(t)
                dve.wait_ge(s_xa, TILES)
                dve.wait_ge(s_fin1_ps, 1)
                link(v.tensor_copy(fin_c[:, 0:3], tiny[:, FIN:FIN + 3]))
                link(v.tensor_tensor(z1[:, :], rows[:, 0, :], xa[:, :], ALU.mult))
                link(v.scalar_tensor_tensor(out=z2[:, :], in0=rows[:, 1, :], scalar=fin_c[:, 0:1], in1=z1[:, :],
                                            op0=ALU.mult, op1=ALU.add))
                link(v.scalar_tensor_tensor(out=z3[:, :], in0=rows[:, 2, :], scalar=fin_c[:, 1:2], in1=z2[:, :],
                                            op0=ALU.mult, op1=ALU.add))
                link(v.tensor_scalar(z3[:, :], z3[:, :], fin_c[:, 2:3], bf, ALU.add, ALU.add))

            for j in range(N2):
                r = slice(ORDER[j] * NB, (ORDER[j] + 1) * NB)
                for m in range(M3):
                    dve.wait_ge(s_h3, M3 * j + m + 1)
                    last = v.bn_stats(h3_stats[:, m, j * BN:(j + 1) * BN], h3T[:, m, r])
                if j == DVE_BLOCKS:
                    z_without_h3()
                if j < DVE_BLOCKS:
                    for m in range(M3):
                        dve.wait_ge(s_h3a, len(banks) + M3 * j + m + 1)
                        if j:
                            dve.wait_ge(s_h3c, M3 * (j - 1) + m + 1)
                        v.tensor_tensor(h3_rest[:, m, :], h3T[:, m, r], h3_part[:, 0, m, r],
                                        ALU.subtract).then_inc(s_h3r, 1)
                    for m in range(M3):
                        dve.wait_ge(s_h3b, M3 * j + m + 1)
                        v.tensor_tensor(h3_part[:, 2, m, r], h3_rest[:, m, :], h3_part[:, 1, m, r],
                                        ALU.subtract).then_inc(s_h3c, 1)
            link(last)
            aggregate(mv3, h3_stats, M3)
            r = inverse_root(6, mv3[:, :, 1], M3)
            link(v.tensor_tensor(a3[:, :], r, g3, ALU.mult))
            link(v.tensor_tensor(a3[:, :], a3[:, :], w_h, ALU.mult))
            link(v.tensor_copy(a3_part[:, :, 0], a3[:, :]))
            link(v.tensor_tensor(a3_rest[:, :], a3[:, :], a3_part[:, :, 0], ALU.subtract))
            link(v.tensor_copy(a3_part[:, :, 1], a3_rest[:, :]))
            link(v.tensor_tensor(a3_part[:, :, 2], a3_rest[:, :], a3_part[:, :, 1], ALU.subtract))
            dve.sem_inc(s_a3, 1)
            link(v.tensor_tensor(fin_h[:, 0, :], mv3[:, :, 0], a3[:, :], ALU.mult))
            link(v.tensor_tensor(fin_h[:, 1, :], e3, w_h, ALU.mult))
            link(v.tensor_tensor(fin_h[:, 2, :], fin_h[:, 1, :], fin_h[:, 0, :], ALU.subtract))
            link(v.reduce_sum(fin_part[:, 0:1], fin_h[:, 2, :], axis=AX.X))
            dve.sem_inc(s_fin_in, 1)
            dve.wait_ge(s_fin_ps, 1)
            dve.wait_ge(s_hd, 1)
            link(v.tensor_copy(fin_c[:, 3:4], tiny[:, FIN + 3:FIN + 4]))
            link(v.reduce_sum(z_h[:, :], tiny[:, HD:HD + 3 * TILES].rearrange("p (t i) -> p t i", i=3), axis=AX.X))
            v.scalar_tensor_tensor(out=z4[:, :], in0=z_h[:, :], scalar=fin_c[:, 3:4], in1=z3[:, :],
                                   op0=ALU.add, op1=ALU.add).then_inc(s_z, 1)

        @block.tensor
        def _(pe):
            mm = nc.tensor.matmul
            pe.sem_inc(s_tp, GROUPS * SLOTS)
            pe.sem_inc(s_acc, 2 * M1)

            def total(asked, n, col, numbers, given):
                pe.wait_ge(asked, n)
                w = numbers.shape[1]
                mm(tiny[:, col:col + w], ones[:, :], numbers, start=True, stop=True).then_inc(given, 1)

            def split_mm(out, w, x, first, last):
                mm(out, w(0), x(0), start=first, stop=False)
                mm(out, w(0), x(1), start=False, stop=False)
                return mm(out, w(1), x(0), start=False, stop=last)

            def shift(out, w, e, kt, mt, s_done):
                for m in range(mt):
                    for k in range(kt):
                        last = mm(out[:, m:m + 1], w[:, k, m * PT:(m + 1) * PT], e[:, k:k + 1],
                                  start=(k == 0), stop=(k == kt - 1))
                last.then_inc(s_done, 1)

            def turn(c, p, i, j, g):
                if g == 0:
                    pe.wait_ge(s_gath[2 * p + j], 16 * NT * (i + 1))
                    pe.wait_ge(s_num[2 * p + j], 16 * (i + 1))
                if not (isinstance(c, int) and c == 0 and j == 0):
                    pe.wait_ge(s_lo, 2 + g + 1 if isinstance(c, int) and c == 0 else GROUPS * (2 * c + j) + g + 1)
                for k in range(width(g)):
                    last = nc.tensor.transpose(tp_bank(c, j, g)[:, k * PT:(k + 1) * PT],
                                               nat[:, 2 * p + j, (GK * g + k) * PT:(GK * g + k + 1) * PT], ident)
                last.then_inc(s_tp, 1)

            def dots(c, p, j, some):
                o = DOT + 8 * j
                for k in some:
                    mm(tiny[:, o:o + 6], xT[:, p, 0, k, j * PT:(j + 1) * PT],
                       al[:, k, :, :].rearrange("p s i -> p (s i)"), start=(k == 0), stop=False)
                    last = mm(tiny[:, o:o + 3], xT[:, p, 1, k, j * PT:(j + 1) * PT], al[:, k, 0, :],
                              start=False, stop=(k == KT - 1))
                if j == 1 and k == KT - 1:
                    last.then_inc(s_dots, 1)

            def spread_rows(c):
                pe.wait_ge(s_rownum, c + 1)
                for row, column in enumerate((p_in, pqt[:, 1, :], pqt[:, 2, :])):
                    for j in range(2):
                        o = (row % 2) * C + j * PT
                        last = nc.tensor.transpose(yb[row // 2][:, o:o + PT],
                                                   column[:, j:j + 1].broadcast_to([PT, PT]), ident)
                last.then_inc(s_bcast, 1)

            def chunk(c, p, other):
                for m in range(M1):
                    pe.wait_ge(s_h1, M1 * c + m + 1)
                    for k in range(KT):
                        if m == 0 and k % GK == 0:
                            pe.wait_ge(s_lo, 2 + GROUPS * (2 * c + 1) + k // GK + 1)
                        if m == 0 and isinstance(c, int) and c == 0:
                            pe.wait_ge(s_w1l, k + 1)
                        if m == 0 and DOTS_AT <= k < DOTS_AT + 2 * GROUPS:
                            j, g = divmod(k - DOTS_AT, GROUPS)
                            if k == DOTS_AT + GROUPS:
                                pe.wait_ge(s_lo, 2 + 2 * GROUPS * (c + 1))
                            dots(c, p, j, range(GK * g, GK * g + width(g)))
                        if KT * m + k == SPREAD_AT:
                            spread_rows(c)
                        other(KT * m + k)
                        if k < KT - 1:
                            split_mm(acc[m % 2][:, 0:C], lambda s: w1[:, k, s, m * PT:(m + 1) * PT],
                                     lambda s: xT[:, p, s, k, :], k == 0, False)
                    for part in range(2):
                        last = mm(acc[m % 2][:, 0:C], w1[:, KT - 1, 0, m * PT:(m + 1) * PT], xT[:, p, part, KT - 1, :],
                                  start=False, stop=(part == 1))
                    last.then_inc(s_acc, 1)

            def next_one(c, p, i_next, schedule):
                sum_at, squares_ahead_of, turn_at = schedule

                def other(t):
                    if t in sum_at:
                        j = sum_at[t]
                        total(s_ask, 2 * (c + 1) + j + 1, SUM_X + j, mx[:, j:j + 1], s_sum)
                    if t in turn_at:
                        turn(c + 1, 1 - p, i_next, *turn_at[t])
                return other

            def later_layers(t):
                if t == SHIFT2_AT:
                    pe.wait_ge(s_w2e, M1 - 1)
                    for m in range(M2):
                        last = mm(turned[:, m:m + 1], w2e[:, m * PT:(m + 1) * PT], ones[:, 0:1], start=True, stop=True)
                    last.then_inc(s_shift2, 1)
                if t == SUM_W2_AT:
                    total(s_wask, 3, SUM_W, mx[:, 2:3], s_wsum)
            pe.wait_ge(s_ones, 1)
            total(s_wask, 1, 0, part1[:, :], s_wsum)
            total(s_wask, 2, SUM_W, mx[:, 2:3], s_wsum)
            pe.wait_ge(s_w1s, 1)
            pe.wait_ge(s_vec, 32)
            pe.wait_ge(s_pad, 2)
            for j in range(2):
                total(s_ask, j + 1, SUM_X + j, mx[:, j:j + 1], s_sum)
                for g in range(GROUPS):
                    turn(0, 0, 0, j, g)
            chunk(0, 0, next_one(0, 0, 0, FIRST))
            with pe.Fori(0, PAIRS - 1) as i:
                chunk(2 * i + 1, 1, next_one(2 * i + 1, 1, i + 1, OTHERS))
                chunk(2 * i + 2, 0, next_one(2 * i + 2, 0, i + 1, OTHERS))
            chunk(CHUNKS - 1, 1, later_layers)

            def spread_weights(some):
                for g in some:
                    if g >= 3:
                        pe.wait_ge(s_arow, g - 2)
                    for k in range(width(g)):
                        last = nc.tensor.transpose(spread_banks[g % 3][:, k * PT:(k + 1) * PT],
                                                   ay[:, GK * g + k:GK * g + k + 1].broadcast_to([PT, PT]), ident)
                    last.then_inc(s_afull, 1)

            def second(j, k, m):
                last = split_mm(banks[m][:, :], lambda s: w2[:, s, k, m * PT:(m + 1) * PT],
                                lambda s: n1_block(j)[:, s, k, :], k == 0, k == M1 - 1)
                if k == M1 - 1:
                    last.then_inc(s_acc2, 1)

            for j in range(N2 - 1):
                for k in range(M1):
                    if j == 1 and k == 0:
                        pe.wait_ge(s_yused, 2 + CHUNKS)
                        pe.wait_ge(s_ay, 1)
                        spread_weights(range(3))
                    if j == 1 and k == 2:
                        spread_weights(range(3, GROUPS))
                    if j == 1 and k == M1 - 2:
                        pe.wait_ge(s_arow, 3)
                        pe.wait_ge(s_w3, 16)
                        shift(turned, w3_raw, e2, M2, M3, s_shift3)
                    if j == 2 and k == M1 // 2:
                        total(s_wask, 4, SUM_W, mx[:, 3:4], s_wsum)
                    if j == 0:
                        pe.wait_ge(s_w2l, k + 1)
                    pe.wait_ge(s_n1l, M1 * j + k + 1)
                    for m in range(M2):
                        if j == 0 and k == 0 and m == 2:
                            pe.wait_ge(s_h1, 2 + M1 * CHUNKS)
                        if k == 0:
                            pe.wait_ge(s_h2, M2 * j + m + 1)
                        second(j, k, m)
            j = N2 - 1
            for m in range(M2):
                pe.wait_ge(s_h2, M2 * j + m + 1)
                for k in range(M1):
                    if m == 0:
                        pe.wait_ge(s_n1l, M1 * j + k + 1)
                    second(j, k, m)
            pe.wait_ge(s_w3s, 1)
            total(s_fin1, 1, FIN, fin_sum[:, 0:3], s_fin1_ps)
            pe.wait_ge(s_w3l, 1)
            pe.wait_ge(s_arow, GROUPS)
            for n, (j, k) in enumerate(L3_STEPS):
                r = slice(ORDER[j] * NB, (ORDER[j] + 1) * NB)
                pe.wait_ge(s_n2l, n + 1)
                for m in range(M3):
                    if k == 0:
                        pe.wait_ge(s_h2 if M3 * j + m < M2 else s_h3a,
                                   M2 * N2 + M3 * j + m + 1 if M3 * j + m < M2 else M3 * j + m + 1)
                    last = split_mm(banks[(M3 * j + m) % len(banks)][:, :],
                                    lambda s: w3[:, s, k, m * PT:(m + 1) * PT],
                                    lambda s: n2[:, s, k, r], k == 0, k == M2 - 1)
                    if k == M2 - 1:
                        last.then_inc(s_acc3, 1)
            pe.wait_ge(s_a3, 1)
            for j in range(N2):
                if j == DVE_BLOCKS:
                    pe.wait_ge(s_h3_last, M3)
                if j == N2 - 1:
                    total(s_fin_in, 1, FIN + 3, fin_part[:, :], s_fin_ps)
                    pe.wait_ge(s_h3_last, M3 * (N2 - DVE_BLOCKS))
                for t in range(ORDER[j] * TILES // N2, (ORDER[j] + 1) * TILES // N2):
                    for m in range(M3):
                        for part in range(3):
                            o = HD + 3 * t
                            last = mm(tiny[:, o:o + 3 - part], h3_part[:, part, m, t * PT:(t + 1) * PT],
                                      a3_part[:, m, 0:3 - part],
                                      start=(m == 0 and part == 0), stop=(m == M3 - 1 and part == 2))
            last.then_inc(s_hd, 1)
            pe.wait_ge(s_z, 1)
            nc.tensor.transpose(turned[0:TILES, 0:PT], z4[:, :], ident).then_inc(s_zT, 1)


def kernel(r_numerical_input, r_categorical_input, L0_rec_emb_tables, L0_rec_cross_alphas, L0_rec_cross_bias,
           L0_rec_w1, L0_rec_b1, L0_rec_g1, L0_rec_be1, L0_rec_w2, L0_rec_b2, L0_rec_g2, L0_rec_be2,
           L0_rec_w3, L0_rec_b3, L0_rec_bn_g, L0_rec_bn_b, L0_rec_wf, L0_rec_bf):
    import numpy as np
    import concourse.bacc as bacc
    from concourse import mybir
    from concourse.bass_utils import run_bass_kernel_spmd

    P = 128

    def columns(v):
        v = np.asarray(v).reshape(-1)
        n = -(-v.shape[0] // P)
        full = np.zeros((n * P,), v.dtype)
        full[:v.shape[0]] = v
        return full.reshape(n, P).T

    def weights(w, twins=False):
        w = np.asarray(w)
        kt = -(-w.shape[1] // P)
        full = np.zeros((kt * P, w.shape[0]), w.dtype)
        full[:w.shape[1]] = w.T
        if twins:
            last = (kt - 1) * P
            full[last + P // 2:last + P // 2 + w.shape[1] - last] = w.T[last:]
        return np.ascontiguousarray(full.reshape(kt, P, w.shape[0]).transpose(1, 0, 2))

    cat = np.asarray(r_categorical_input)
    tables = np.ascontiguousarray(L0_rec_emb_tables)
    nt, v_rows, e = tables.shape
    d = L0_rec_w1.shape[1]
    alphas = np.stack([columns(a) for a in np.asarray(L0_rec_cross_alphas)], axis=2).reshape(P, -1)
    bias = [columns(b) for b in np.asarray(L0_rec_cross_bias)]
    bn_g, bn_b, wf = (np.asarray(a).reshape(-1) for a in (L0_rec_bn_g, L0_rec_bn_b, L0_rec_wf))
    vec = [alphas, *bias, columns(bn_g[:d]), columns(bn_b[:d]), columns(wf[:d]),
           columns(L0_rec_b1), columns(L0_rec_g1), columns(L0_rec_be1),
           columns(L0_rec_b2), columns(L0_rec_g2), columns(L0_rec_be2),
           columns(L0_rec_b3), columns(bn_g[d:]), columns(bn_b[d:]), columns(wf[d:]), columns(L0_rec_bf)]
    base = np.broadcast_to(np.arange(nt, dtype=np.float32) * v_rows, (P, nt))
    arrays = {
        "cat": np.ascontiguousarray(cat.reshape(-1, P, nt).transpose(1, 0, 2)),
        "num": np.ascontiguousarray(r_numerical_input),
        "table": tables,
        "vec": np.ascontiguousarray(np.concatenate(vec, axis=1)),
        "const": np.ascontiguousarray(np.concatenate([np.eye(P, dtype=np.float32), base], axis=1)),
        "w1t": weights(L0_rec_w1, twins=True), "w2t": weights(L0_rec_w2), "w3t": weights(L0_rec_w3),
    }
    nc = bacc.Bacc("TRN2", target_bir_lowering=False, num_devices=1)
    args = [nc.dram_tensor(name, a.shape, mybir.dt.from_np(a.dtype), kind="ExternalInput").ap()
            for name, a in arrays.items()]
    out = nc.dram_tensor("out", (cat.shape[0], 1), mybir.dt.float32, kind="ExternalOutput").ap()
    wide_cross_mlp(nc, *args, out)
    return run_bass_kernel_spmd(nc, [arrays], core_ids=[0]).results[0]["out"]
```
